# Optimizing a Trainium2 kernel written in Bass

```python
import numpy as np
import jax
import jax.numpy as jnp

def _softmax(x, axis=-1):
    return jax.nn.softmax(x, axis=axis)
def _gelu(x):
    return jax.nn.gelu(x, approximate=True)
def _silu(x):
    return jax.nn.silu(x)
def _sigmoid(x):
    return jax.nn.sigmoid(x)
def _layernorm(x, axis=-1, eps=1e-5):
    m = jnp.mean(x, axis=axis, keepdims=True)
    v = jnp.var(x, axis=axis, keepdims=True)
    return (x - m) / jnp.sqrt(v + eps)
def _scatter_add(tgt, idx, src, axis=0):
    return tgt.at[idx].add(src)
def _segment_sum(src, seg, n):
    return jax.ops.segment_sum(src, seg, n)

kernel_name = 'mk_conv_preact_d1_conv_nhwc256_26b083'

def setup_inputs(seed: int = 0):
    np.random.seed(seed)
    _w = jnp.asarray
    def _rec_inputs():
        import jax
        import jax.numpy as jnp
        _gk = jax.random.key(seed)
        x = -0.0003957 + 1 * jax.random.normal(jax.random.fold_in(_gk, 1), (16, 56, 56, 256), jnp.float32)
        return x
    x = _rec_inputs()
    def _L0_conv_setup():
        import jax, jax.numpy as jnp
        import numpy as np

        def _threshold(w):
            return 0.7 * jnp.mean(jnp.abs(w))

        def _compute_alpha(w):
            t = _threshold(w)
            kept = jnp.where(w > t, w, 0.0) + jnp.where(w < -t, w, 0.0)
            kept_abs = jnp.abs(kept)
            n = jnp.sum((kept_abs > 0).astype(w.dtype))
            return jnp.sum(kept_abs) / n

        def _ternary(w):
            t = _threshold(w)
            return jnp.sign(jnp.sign(w + t) + jnp.sign(w - t))
        key = jax.random.key(seed)
        k1, k2 = jax.random.split(key)
        x = jax.random.normal(k1, (16, 56, 56, 256), dtype=jnp.float32)
        W = jax.random.normal(k2, (3, 3, 256, 256), dtype=jnp.float32) * 0.02
        b = jnp.zeros((256,), dtype=jnp.float32)
        return {'x': x, 'W': W, 'b': b}
    _L0_conv_all = _L0_conv_setup()
    _L0_conv_in = {k: v for k, v in _L0_conv_all.items() if k in ('W', 'b', )}
    del _L0_conv_all

    return {
        "x": x,
        "L0_conv_W": _L0_conv_in["W"],
        "L0_conv_b": _L0_conv_in["b"],
    }

def reference(x, L0_conv_W, L0_conv_b):
    import jax
    import jax.numpy as jnp
    def _L0_conv_ref(x, W, b):
        import jax, jax.numpy as jnp
        import numpy as np

        def _threshold(w):
            return 0.7 * jnp.mean(jnp.abs(w))

        def _compute_alpha(w):
            t = _threshold(w)
            kept = jnp.where(w > t, w, 0.0) + jnp.where(w < -t, w, 0.0)
            kept_abs = jnp.abs(kept)
            n = jnp.sum((kept_abs > 0).astype(w.dtype))
            return jnp.sum(kept_abs) / n

        def _ternary(w):
            t = _threshold(w)
            return jnp.sign(jnp.sign(w + t) + jnp.sign(w - t))
        alpha = _compute_alpha(W)
        w_q = alpha * _ternary(W)
        y = jax.lax.conv_general_dilated(x, w_q, window_strides=(1, 1), padding='SAME', dimension_numbers=('NHWC', 'HWIO', 'NHWC'))
        return jax.nn.relu(y + b)

    def _gn(v, G=32, eps=1e-5):
        B_, H_, W_, C_ = v.shape
        g = v.reshape(B_, H_, W_, G, C_ // G)
        m = jnp.mean(g, axis=(1, 2, 4), keepdims=True)
        s = jnp.var(g, axis=(1, 2, 4), keepdims=True)
        return ((g - m) / jnp.sqrt(s + eps)).reshape(v.shape)

    def _ln_c(v, eps=1e-6):
        m = jnp.mean(v, axis=-1, keepdims=True)
        s = jnp.var(v, axis=-1, keepdims=True)
        return (v - m) / jnp.sqrt(s + eps)

    def _ln_t(v, eps=1e-5):
        m = jnp.mean(v, axis=-1, keepdims=True)
        s = jnp.var(v, axis=-1, keepdims=True)
        return (v - m) / jnp.sqrt(s + eps)

    def _to_tokens(v):
        B_, H_, W_, C_ = v.shape
        return v.reshape(B_, H_ * W_, C_)
    def _from_tokens(t, like):
        return t.reshape(like.shape)

    x = x + _L0_conv_ref(_gn(x), L0_conv_W, L0_conv_b)
    return x


_drawn_inputs = setup_inputs


def setup_inputs(seed=0):
    import zlib

    import numpy as np

    out = dict(_drawn_inputs(seed))
    spreads = {'L0_conv_b': (0.0, 0.1)}
    factors = {}
    for name, (base, spread) in spreads.items():
        noise = np.random.default_rng([zlib.crc32(name.encode()), seed]).standard_normal(out[name].shape)
        drawn = base * np.exp(spread * noise) if base else spread * noise
        out[name] = jnp.asarray(drawn.astype(out[name].dtype))
    for name, factor in factors.items():
        out[name] = (out[name] * factor).astype(out[name].dtype)
    return out
```

```python
from contextlib import ExitStack

import concourse.bass as bass
from concourse import mybir

F32 = mybir.dt.float32
F16 = mybir.dt.float16
ALU = mybir.AluOpType
ACT = mybir.ActivationFunctionType

BATCH, ROWS, COLS, CH = 16, 56, 56, 256
KH, KW = 3, 3
P = 128
HALVES = CH // P
GROUP_CH = CH // 32
EPS = 1e-5
THRESHOLD = 0.7
SPLIT_SCALE = 128.0

QUARTERS = 4
UNITS = BATCH * QUARTERS
UROWS = ROWS // QUARTERS
PAIRS = UROWS // 2
NPOS = PAIRS * COLS
BLOCK = 2 * COLS
BLOCKS = UROWS // 2
BATCHES = ((0, 4), (4, 3))
PCOLS = COLS + 2
TROWS = 4 * PAIRS
BANK = 512

XSLOTS = 8
ZSLOTS = 4
LEAD = 5
FILTER = (1, 2, 0, 3)
FIRST_ROW = (0, 2 * PAIRS, 3 * PAIRS, 1)
ROW_STEP = (2, 1, 1, 2)
TIN_GAPS = (0, 1, 2, 3)
TOUT_GAPS = ((5, 7), (1, 3))
MEAN_GAP, VAR_GAP = 5, 7
CHAIN = 8


def build(nc, x, w, b, out):
    x_units = x.rearrange("n h w c -> (n h w) c").rearrange("(u t p) c -> u p t c", t=BLOCKS, p=BLOCK)
    out_units = out.rearrange("n h w c -> (n h w) c").rearrange("(u t p) c -> u p t c", t=BLOCKS, p=BLOCK)
    n_weights = KH * KW * CH * CH
    w_len = n_weights // P

    with ExitStack() as ctx:
        def sb(name, shape, dt=F32):
            return ctx.enter_context(nc.sbuf_tensor(name, shape, dt))

        def ps(name, shape):
            return ctx.enter_context(nc.psum_tensor(name, shape, F32))

        def sem(name):
            return ctx.enter_context(nc.semaphore(name))

        x_nat = sb("x_nat", [P, XSLOTS, BLOCKS, CH])
        xT = sb("xT", [P, 2, HALVES, ROWS + 2, COLS])
        U = sb("U", [P, HALVES, TROWS, COLS])
        Z = sb("Z", [P, ZSLOTS, 2, HALVES, TROWS, PCOLS], F16)
        Y = sb("Y", [P, 2, UROWS * COLS])
        AB = sb("AB", [P, 2, NPOS])
        m1_sb = sb("m1_sb", [P, NPOS])
        filt = sb("filt", [P, 4, KW, HALVES, CH], F16)
        ident = sb("ident", [P, P])
        ones = sb("ones", [P, P])
        group_avg = sb("group_avg", [P, P])
        bias = sb("bias", [P, HALVES])
        part_sums = sb("part_sums", [P, HALVES, QUARTERS * 2, 6])
        ch_stats = sb("ch_stats", [P, HALVES, 2])
        mean = sb("mean", [P, HALVES])
        neg2mean = sb("neg2mean", [P, HALVES])
        dev = sb("dev", [P, HALVES])
        spread = sb("spread", [P, HALVES])
        var = sb("var", [P, HALVES])
        std = sb("std", [P, HALVES])
        inv0 = sb("inv0", [P, HALVES])
        corr = sb("corr", [P, HALVES])
        scale = sb("scale", [P, HALVES])
        w_sum = sb("w_sum", [P, 1])
        thr = sb("thr", [P, 1])
        neg_thr = sb("neg_thr", [P, 1])
        kept = sb("kept", [P, 2])
        kept_all = sb("kept_all", [P, 2])
        inv_n = sb("inv_n", [P, 1])
        alpha = sb("alpha", [P, 1])

        w_raw = x_nat[:, 5:8].rearrange("p s t c -> p (s t c)")[:, 0:w_len]
        w_abs = xT[:, 1].rearrange("p h r c -> p (h r c)")[:, 0:w_len]
        w_neg = Z[:, 2].rearrange("p a h r c -> p (a h r c)")[:, 0:w_len]
        w_ter = Z[:, 3].rearrange("p a h r c -> p (a h r c)")[:, 0:w_len]
        tern = w_ter.rearrange("p (k n) -> p k n", k=KH)
        tap_sum = w_neg[:, 0:w_len // KH]

        M1 = ps("M1", [P, BANK])
        M2 = ps("M2", [P, BANK])
        M03 = ps("M03", [P, 2, 2, BANK])
        tin = ps("tin", [P, BANK])
        tout = ps("tout", [P, BANK])

        w_loaded = sem("w_loaded")
        b_loaded = sem("b_loaded")
        x_loaded = [sem(f"x_loaded{i}") for i in range(XSLOTS)]
        x_stored = sem("x_stored")
        consts_made = sem("consts_made")
        pads_made = sem("pads_made")
        w_abs_made = sem("w_abs_made")
        w_sums = sem("w_sums")
        w_step = sem("w_step")
        tin_done = sem("tin_done")
        xt_evac = sem("xt_evac")
        bn_done = sem("bn_done")
        ch_stats_ready = sem("ch_stats_ready")
        group_sums = sem("group_sums")
        spread_ready = sem("spread_ready")
        var_read = sem("var_read")
        std_made = sem("std_made")
        stat_step = sem("stat_step")
        u_made = sem("u_made")
        hi_made = sem("hi_made")
        lo_made = sem("lo_made")
        mm_done = sem("mm_done")
        m1_copied = sem("m1_copied")
        ab_made = sem("ab_made")
        y_made = sem("y_made")
        relu_made = sem("relu_made")
        tout_done = sem("tout_done")
        added = sem("added")

        block = ctx.enter_context(nc.Block())

        def present(s, inside):
            if inside:
                return True, True, True, True
            return s + LEAD < UNITS, 0 <= s + 1 < UNITS, 0 <= s < UNITS, s >= 1

        @block.sync
        def _(sp):
            sp.dma_start(w_raw.rearrange("p (k c) -> p k c", c=CH),
                         w.rearrange("a b (k p) c -> p (a b k) c", p=P)).then_inc(w_loaded, 16)
            for u in range(XSLOTS):
                if u == 5:
                    sp.wait_ge(w_step, 5)
                sp.dma_start(x_nat[0:BLOCK, u], x_units[u]).then_inc(x_loaded[u], 16)

            def store(s, slot):
                sp.wait_ge(added, 4 * s + 4)
                sp.dma_start(out_units[s], x_nat[0:BLOCK, slot]).then_inc(x_stored, 16)
                sp.wait_ge(x_stored, 16 * s + 16)

            with sp.Fori(0, UNITS // XSLOTS - 1) as k:
                for slot in range(XSLOTS):
                    store(k * XSLOTS + slot, slot)
                    sp.dma_start(x_nat[0:BLOCK, slot], x_units[k * XSLOTS + (slot + XSLOTS)]
                                 ).then_inc(x_loaded[slot], 16)
            for s in range(UNITS - XSLOTS, UNITS):
                store(s, s % XSLOTS)

        @block.gpsimd
        def _(pool):
            pool.dma_start(bias[:, :], b.rearrange("(h p) -> p h", p=P),
                           allow_slow_non_contiguous=True).then_inc(b_loaded, 16)
            pool.memset(ones[:, :], 1.0).then_inc(consts_made, 1)
            pool.memset(ident[:, :], 0.0).then_inc(consts_made, 1)
            pool.memset(group_avg[:, :], 1.0 / GROUP_CH).then_inc(consts_made, 1)
            pool.memset(Z[:, 0:2, :, :, :, 0:PCOLS:PCOLS - 1].rearrange("p s a h r c -> p (s a h r) c"),
                        0.0).then_inc(pads_made, 1)
            pool.wait_ge(consts_made, 3)
            pool.affine_select(out=ident[:, :], in_=ident[:, :], compare_op=ALU.not_equal, fill=1.0, base=0,
                               pattern=[[-1, P]], channel_multiplier=1).then_inc(consts_made, 1)
            g_view = group_avg[:, :].rearrange("p (g e) -> p g e", e=GROUP_CH)
            pool.affine_select(out=g_view, in_=g_view, compare_op=ALU.is_ge, fill=0.0, base=0,
                               pattern=[[-GROUP_CH, P // GROUP_CH], [0, GROUP_CH]],
                               channel_multiplier=1).then_inc(consts_made, 1)
            pool.wait_ge(consts_made, 5)
            pool.affine_select(out=g_view, in_=g_view, compare_op=ALU.is_ge, fill=0.0, base=GROUP_CH - 1,
                               pattern=[[GROUP_CH, P // GROUP_CH], [0, GROUP_CH]],
                               channel_multiplier=-1).then_inc(consts_made, 1)
            pool.wait_ge(w_step, 11)
            pool.memset(Z[:, 2:4, :, :, :, 0:PCOLS:PCOLS - 1].rearrange("p s a h r c -> p (s a h r) c"),
                        0.0).then_inc(pads_made, 1)

        @block.scalar
        def _(act):
            act.wait_ge(w_loaded, 16)
            act.activation(w_abs, w_raw, ACT.Abs, accum_out=w_sum[:, :]).then_inc(w_abs_made, 1)

            def evacuate(u, j, n):
                half, (first, count) = n // 2, BATCHES[n % 2]
                t, par = j % QUARTERS, j // QUARTERS % 2
                act.wait_ge(tin_done, 4 * u + n + 1)
                if t == 0 and n == 0 and not (type(u) is int and u < 2 * QUARTERS):
                    act.wait_ge(u_made, 2 * u - 2 * QUARTERS)
                if type(u) is int and u == QUARTERS and n == 0:
                    act.wait_ge(w_step, 8)
                row = 1 + UROWS * t + 2 * first
                act.activation(xT[:, par, half, row:row + 2 * count, :].rearrange("p r c -> p (r c)"),
                               tin[:, 0:count * BLOCK], ACT.Copy).then_inc(xt_evac, 1)

            def high(v, j, half):
                slot = j % ZSLOTS
                act.wait_ge(u_made, 2 * v + half + 1)
                if half == 0:
                    if type(v) is int and v < 2:
                        act.wait_ge(pads_made, 1)
                    else:
                        act.wait_ge(pads_made, 2)
                        act.wait_ge(mm_done, 8 * v - 15)
                act.activation(Z[:, slot, 0, half, :, 1:COLS + 1], U[:, half], ACT.Copy,
                               scale=scale[:, half:half + 1]).then_inc(hi_made, 1)

            def copy_m1(s, c):
                act.wait_ge(mm_done, 8 * s + 4 * c + 1)
                if not (type(s) is int and 2 * s + c < 1):
                    act.wait_ge(ab_made, 2 * s + c)
                act.activation(m1_sb[:, :], M1[:, 0:NPOS], ACT.Copy).then_inc(m1_copied, 1)

            def relu(s, c):
                act.wait_ge(y_made, 2 * s + c + 1)
                act.activation(Y[:, c], Y[:, c], ACT.Relu, bias=bias[:, c:c + 1],
                               scale=alpha[:, :]).then_inc(relu_made, 1)

            def step(s, j, inside=False):
                do_tin, do_tr, do_mm, do_end = present(s, inside)
                if do_end:
                    relu(s - 1, 1)
                if do_tr and (j + 1) % QUARTERS == 0:
                    m4 = s + 1
                    act.wait_ge(var_read, (j_image(m4) + 1) if type(s) is int else image_of(s, j + 1) + 1)
                    act.activation(std[:, :], var[:, :], ACT.Sqrt).then_inc(std_made, 1)
                if do_tin:
                    evacuate(s + LEAD, j + LEAD, 0)
                if do_mm:
                    copy_m1(s, 0)
                if do_tr:
                    high(s + 1, j + 1, 0)
                if do_tin:
                    for n in (1, 2, 3):
                        evacuate(s + LEAD, j + LEAD, n)
                if do_mm:
                    if s_is(s, 0):
                        act.wait_ge(b_loaded, 16)
                        act.wait_ge(w_step, 14)
                    relu(s, 0)
                    copy_m1(s, 1)
                if do_tr:
                    high(s + 1, j + 1, 1)

            def s_is(s, n):
                return type(s) is int and s == n

            def j_image(n):
                return n // QUARTERS

            def image_of(s, j):
                return images[0] * 2 + j // QUARTERS

            images = [None]

            for s in range(-LEAD, 1):
                step(s, s)
            with act.Fori(0, (UNITS - 8) // 8) as k:
                images[0] = k
                for j in range(1, 9):
                    step(k * 8 + j, j, True)
            for s in range(UNITS - 7, UNITS + 1):
                step(s, s)

        @block.vector
        def _(dve):
            dve.wait_ge(w_sums, 1)
            dve.tensor_scalar(thr[:, :], tout[:, 0:1], 1.0 / n_weights, THRESHOLD, ALU.mult, ALU.mult
                              ).then_inc(w_step, 1)
            dve.wait_ge(w_step, 1)
            dve.tensor_scalar(neg_thr[:, :], thr[:, :], -1.0, None, ALU.mult).then_inc(w_step, 1)
            dve.wait_ge(w_step, 2)
            dve.tensor_scalar(w_neg, w_raw, neg_thr[:, :], None, ALU.is_le).then_inc(w_step, 2)
            dve.wait_ge(w_step, 4)
            dve.scalar_tensor_tensor(w_ter, w_raw, thr[:, :], w_neg, ALU.is_ge, ALU.subtract
                                     ).then_inc(w_step, 1)
            dve.wait_ge(w_step, 5)
            flat = [filt[:, i].rearrange("p k h c -> p (k h c)") for i in range(4)]
            dve.tensor_tensor(tap_sum, tern[:, 0], tern[:, 2], ALU.add).then_inc(w_step, 1)
            dve.wait_ge(w_abs_made, 1)
            dve.scalar_tensor_tensor(w_abs, w_abs, thr[:, :], w_abs, ALU.is_gt, ALU.mult,
                                     accum_out=kept[:, 1:2]).then_inc(w_step, 1)
            dve.wait_ge(w_step, 7)
            dve.tensor_scalar(w_abs, w_abs, 0.0, None, ALU.is_gt, ALU.add, accum_out=kept[:, 0:1]
                              ).then_inc(w_step, 1)
            dve.tensor_scalar(tap_sum, tap_sum, 0.5, None, ALU.mult).then_inc(w_step, 1)
            dve.tensor_scalar(flat[0], tern[:, 0], -1.0, None, ALU.mult)
            dve.tensor_copy(flat[3], tern[:, 2])
            dve.wait_ge(w_step, 9)
            dve.scalar_tensor_tensor(flat[1], tern[:, 1], 0.5, tap_sum, ALU.mult, ALU.add).then_inc(w_step, 1)
            dve.scalar_tensor_tensor(flat[2], tern[:, 1], -0.5, tap_sum, ALU.mult, ALU.add).then_inc(w_step, 1)

            def make_alpha():
                dve.wait_ge(w_sums, 2)
                dve.tensor_copy(kept_all[:, :], tout[:, 2:4]).then_inc(w_step, 1)
                dve.wait_ge(w_step, 12)
                dve.reciprocal(inv_n[:, :], kept_all[:, 0:1]).then_inc(w_step, 1)
                dve.wait_ge(w_step, 13)
                dve.scalar_tensor_tensor(alpha[:, :], kept_all[:, 1:2], 1.0 / SPLIT_SCALE, inv_n[:, :],
                                         ALU.mult, ALU.mult).then_inc(w_step, 1)

            def partial_stats(u, j, n):
                half, (first, count) = n // 2, BATCHES[n % 2]
                t, par = j % QUARTERS, j // QUARTERS % 2
                dve.wait_ge(xt_evac, 4 * u + n + 1)
                row = 1 + UROWS * t + 2 * first
                dve.bn_stats(part_sums[:, half, 2 * t + n % 2],
                             xT[:, par, half, row:row + 2 * count, :].rearrange("p r c -> p (r c)")
                             ).then_inc(bn_done, 1)

            def channel_stats():
                for half in range(HALVES):
                    ins = dve.bn_aggr(ch_stats[:, half], part_sums[:, half].rearrange("p n k -> p (n k)"))
                ins.then_inc(ch_stats_ready, 1)

            def group_mean(m):
                at = m * CHAIN
                dve.wait_ge(group_sums, 2 * m + 1)
                dve.tensor_copy(mean[:, :], tin[:, 0:HALVES]).then_inc(stat_step, 1)
                dve.wait_ge(stat_step, at + 1)
                dve.tensor_tensor(dev[:, :], ch_stats[:, :, 0], mean[:, :], ALU.subtract).then_inc(stat_step, 1)
                dve.wait_ge(stat_step, at + 2)
                dve.tensor_tensor(spread[:, :], dev[:, :], dev[:, :], ALU.mult).then_inc(stat_step, 1)
                dve.tensor_scalar(neg2mean[:, :], mean[:, :], -2.0, None, ALU.mult)
                dve.wait_ge(stat_step, at + 3)
                dve.tensor_tensor(spread[:, :], spread[:, :], ch_stats[:, :, 1], ALU.add).then_inc(spread_ready, 1)

            def group_var(m):
                dve.wait_ge(group_sums, 2 * m + 2)
                dve.tensor_scalar(var[:, :], tin[:, 8:8 + HALVES], EPS, None, ALU.add).then_inc(var_read, 1)

            def group_scale(m, par):
                at = m * CHAIN
                for half in range(HALVES):
                    dve.tensor_scalar(xT[:, par, half, 0:ROWS + 2:ROWS + 1, :],
                                      ones[:, 0:2 * COLS].rearrange("p (r c) -> p r c", r=2),
                                      mean[:, half:half + 1], None, ALU.mult)
                dve.wait_ge(std_made, m + 1)
                dve.reciprocal(inv0[:, :], std[:, :]).then_inc(stat_step, 1)
                dve.wait_ge(stat_step, at + 4)
                dve.tensor_tensor(corr[:, :], inv0[:, :], inv0[:, :], ALU.mult).then_inc(stat_step, 1)
                dve.wait_ge(stat_step, at + 5)
                dve.tensor_tensor(corr[:, :], corr[:, :], var[:, :], ALU.mult).then_inc(stat_step, 1)
                dve.wait_ge(stat_step, at + 6)
                dve.tensor_scalar(corr[:, :], corr[:, :], -0.5 * SPLIT_SCALE, 1.5 * SPLIT_SCALE,
                                  ALU.mult, ALU.add).then_inc(stat_step, 1)
                dve.wait_ge(stat_step, at + 7)
                dve.tensor_tensor(scale[:, :], corr[:, :], inv0[:, :], ALU.mult).then_inc(stat_step, 1)
                dve.wait_ge(stat_step, at + 8)

            def transform(j, half):
                t, par = j % QUARTERS, j // QUARTERS % 2
                row = UROWS * t
                src, dst = xT[:, par, half], U[:, half]
                dve.tensor_tensor(dst[:, 0:UROWS].rearrange("p r c -> p (r c)"),
                                  src[:, row + 2:row + 2 + UROWS].rearrange("p r c -> p (r c)"),
                                  src[:, row:row + UROWS].rearrange("p r c -> p (r c)"), ALU.subtract)
                even, odd = src[:, row + 1:row + 1 + UROWS:2], src[:, row + 2:row + 2 + UROWS:2]
                dve.scalar_tensor_tensor(dst[:, UROWS:UROWS + PAIRS], even, neg2mean[:, half:half + 1], odd,
                                         ALU.add, ALU.add)
                dve.tensor_tensor(dst[:, UROWS + PAIRS:TROWS], odd, even, ALU.subtract).then_inc(u_made, 1)

            def low(v, j, half):
                slot = j % ZSLOTS
                dve.wait_ge(hi_made, 2 * v + half + 1)
                dve.scalar_tensor_tensor(Z[:, slot, 1, half, :, 1:COLS + 1], U[:, half],
                                         scale[:, half:half + 1], Z[:, slot, 0, half, :, 1:COLS + 1],
                                         ALU.mult, ALU.subtract).then_inc(lo_made, 1)

            def sum_and_difference(s, c):
                dve.wait_ge(m1_copied, 2 * s + c + 1)
                dve.wait_ge(mm_done, 8 * s + 4 * c + 2)
                dve.tensor_tensor(AB[:, 0], m1_sb[:, :], M2[:, 0:NPOS], ALU.add)
                dve.tensor_tensor(AB[:, 1], m1_sb[:, :], M2[:, 0:NPOS], ALU.subtract).then_inc(ab_made, 1)

            def join(s, c, first=False):
                dve.wait_ge(mm_done, 8 * s + 4 * c + 4)
                dve.wait_ge(ab_made, 2 * s + c + 1)
                if c == 1:
                    dve.wait_ge(tout_done, 4 * s + 1)
                elif not first:
                    dve.wait_ge(tout_done, 4 * s - 2)
                dve.tensor_tensor(Y[:, c].rearrange("p (r j c) -> p j r c", j=2, c=COLS),
                                  AB[:, :].rearrange("p j (r c) -> p j r c", c=COLS),
                                  M03[:, c, :, 0:NPOS].rearrange("p j (r c) -> p j r c", c=COLS),
                                  ALU.add).then_inc(y_made, 1)

            def add_residual(s, j, c, n):
                first, count = BATCHES[n]
                dve.wait_ge(tout_done, 4 * s + 2 * c + n + 1)
                dst = x_nat[0:BLOCK, j % XSLOTS, first:first + count, c * P:(c + 1) * P]
                dve.tensor_tensor(dst, dst, tout[0:BLOCK, 0:count * P].rearrange("p (t c) -> p t c", c=P),
                                  ALU.add).then_inc(added, 1)

            def step(s, j, image, inside=False):
                do_tin, do_tr, do_mm, do_end = present(s, inside)
                u, v = s + LEAD, s + 1
                last_quarter = do_tin and (j + LEAD) % QUARTERS == QUARTERS - 1
                if do_end:
                    join(s - 1, 1)
                    add_residual(s - 1, j - 1, 0, 1)
                if do_tr and (j + 1) % QUARTERS == 0:
                    m = image(j + 1)
                    group_var(m)
                    group_scale(m, (j + 1) // QUARTERS % 2)
                if do_tr:
                    transform(j + 1, 0)
                if do_tin:
                    partial_stats(u, j + LEAD, 0)
                if do_mm:
                    sum_and_difference(s, 0)
                if do_end:
                    add_residual(s - 1, j - 1, 1, 0)
                if do_tin:
                    partial_stats(u, j + LEAD, 1)
                if do_tr:
                    low(v, j + 1, 0)
                if do_tin:
                    partial_stats(u, j + LEAD, 2)
                if do_mm:
                    join(s, 0, first=type(s) is int and s == 0)
                if do_end:
                    add_residual(s - 1, j - 1, 1, 1)
                if do_tin:
                    partial_stats(u, j + LEAD, 3)
                if last_quarter:
                    dve.wait_ge(bn_done, 4 * u + 4)
                if do_tr:
                    transform(j + 1, 1)
                if last_quarter:
                    channel_stats()
                if do_mm:
                    sum_and_difference(s, 1)
                if last_quarter:
                    group_mean(image(j + 2))
                if do_mm:
                    add_residual(s, j, 0, 0)
                if do_tr:
                    low(v, j + 1, 1)

            for s in range(-LEAD, 1):
                if s == 0:
                    make_alpha()
                step(s, s, lambda n: n // QUARTERS)
            with dve.Fori(0, (UNITS - 8) // 8) as k:
                for j in range(1, 9):
                    step(k * 8 + j, j, lambda n: k * 2 + n // QUARTERS, True)
            for s in range(UNITS - 7, UNITS + 1):
                step(s, s, lambda n: n // QUARTERS)

        @block.tensor
        def _(pe):
            pe.wait_ge(consts_made, 1)
            pe.wait_ge(w_abs_made, 1)
            pe.matmul(tout[:, 0:1], ones[:, :], w_sum[:, :], start=True, stop=True).then_inc(w_sums, 1)
            pe.wait_ge(consts_made, 6)

            def transpose_x(u, j, n):
                half, (first, count) = n // 2, BATCHES[n % 2]
                if n == 0:
                    slot = j % XSLOTS
                    pe.wait_ge(x_loaded[slot], 16 * load_round[0] + 16)
                if not (type(u) is int and u == 0 and n == 0):
                    pe.wait_ge(xt_evac, 4 * u + n)
                if j % QUARTERS == 0 and n == 0 and not (type(u) is int and u == 0):
                    pe.wait_ge(var_read, stats_read[0])
                for i in range(count):
                    ins = pe.transpose(tin[:, i * BLOCK:(i + 1) * BLOCK],
                                       x_nat[0:BLOCK, j % XSLOTS, first + i, half * P:(half + 1) * P],
                                       ident[0:BLOCK, 0:BLOCK])
                ins.then_inc(tin_done, 1)

            load_round = [0]
            stats_read = [0]

            def transpose_y(s, c, n):
                first, count = BATCHES[n]
                if n == 0:
                    pe.wait_ge(relu_made, 2 * s + c + 1)
                if not (type(s) is int and 4 * s + 2 * c + n == 0):
                    pe.wait_ge(added, 4 * s + 2 * c + n)
                for i in range(count):
                    ins = pe.transpose(tout[0:BLOCK, i * P:(i + 1) * P],
                                       Y[:, c, (first + i) * BLOCK:(first + i + 1) * BLOCK], ident[:, :])
                ins.then_inc(tout_done, 1)

            def product(s, j, c, i):
                past = 2 * s + c
                if i == 1:
                    target = M1[:, 0:NPOS]
                    free, count = m1_copied, past
                elif i == 2:
                    target = M2[:, 0:NPOS]
                    free, count = ab_made, past
                else:
                    target = M03[:, c, i // 3, 0:NPOS]
                    free, count = y_made, past - 1
                if i != 3 and not (type(count) is int and count < 1):
                    pe.wait_ge(free, count)
                n = 0
                for kw in range(KW):
                    for half in range(HALVES):
                        for part in range(2):
                            first, row_step = FIRST_ROW[i], ROW_STEP[i]
                            ins = pe.matmul(target, filt[:, i, kw, half, c * P:(c + 1) * P],
                                            Z[:, j % ZSLOTS, part, half,
                                              first:first + row_step * (PAIRS - 1) + 1:row_step, kw:kw + COLS],
                                            start=n == 0, stop=n == 2 * KW * HALVES - 1)
                            n += 1
                ins.then_inc(mm_done, 1)

            def step(s, j, image, inside=False):
                do_tin, do_tr, do_mm, do_end = present(s, inside)
                load_round[0] = image(j + LEAD, 2 * QUARTERS)
                stats_read[0] = image(j + LEAD, QUARTERS)
                last_quarter = do_tin and (j + LEAD) % QUARTERS == QUARTERS - 1
                if do_mm:
                    pe.wait_ge(hi_made, 2 * s + 2)
                    pe.wait_ge(lo_made, 2 * s + 2)
                for g in range(8):
                    if do_mm:
                        product(s, j, g // 4, FILTER[g % 4])
                    if do_tin and g in TIN_GAPS:
                        transpose_x(s + LEAD, j + LEAD, TIN_GAPS.index(g))
                    if do_end and g in TOUT_GAPS[1]:
                        transpose_y(s - 1, 1, TOUT_GAPS[1].index(g))
                    if do_mm and g in TOUT_GAPS[0]:
                        transpose_y(s, 0, TOUT_GAPS[0].index(g))
                    if last_quarter and g == MEAN_GAP:
                        m = image(j + 2, QUARTERS)
                        pe.wait_ge(ch_stats_ready, m + 1)
                        pe.wait_ge(xt_evac, 16 * m + 16)
                        pe.matmul(tin[:, 0:HALVES], group_avg[:, :], ch_stats[:, :, 0],
                                  start=True, stop=True).then_inc(group_sums, 1)
                    if last_quarter and g == VAR_GAP:
                        m = image(j + 2, QUARTERS)
                        pe.wait_ge(spread_ready, m + 1)
                        pe.matmul(tin[:, 8:8 + HALVES], group_avg[:, :], spread[:, :],
                                  start=True, stop=True).then_inc(group_sums, 1)
                if type(s) is int and s == -1:
                    pe.wait_ge(w_step, 11)
                    pe.matmul(tout[:, 2:4], ones[:, :], kept[:, :], start=True, stop=True).then_inc(w_sums, 1)

            for s in range(-LEAD, 1):
                step(s, s, lambda n, size: n // size)
            with pe.Fori(0, (UNITS - 8) // 8) as k:
                for j in range(1, 9):
                    step(k * 8 + j, j, lambda n, size: k * (8 // size) + n // size, True)
            for s in range(UNITS - 7, UNITS + 1):
                step(s, s, lambda n, size: n // size)


def kernel(x, L0_conv_W, L0_conv_b):
    import numpy as _np
    import concourse.bacc as _bacc
    from concourse.bass_utils import run_bass_kernel_spmd as _run

    nc = _bacc.Bacc("TRN2", target_bir_lowering=False, num_devices=1)
    arrays, args = {}, []
    for name, a in (("x", x), ("w", L0_conv_W), ("b", L0_conv_b)):
        a = _np.ascontiguousarray(a)
        arrays[name] = a
        args.append(nc.dram_tensor(name, a.shape, mybir.dt.from_np(a.dtype), kind="ExternalInput").ap())
    args.append(nc.dram_tensor("out", arrays["x"].shape, F32, kind="ExternalOutput").ap())
    build(nc, *args)
    return _run(nc, [arrays], core_ids=[0]).results[0]["out"]
```

```python
from contextlib import ExitStack

import concourse.bass as bass
from concourse import mybir

F32 = mybir.dt.float32
F16 = mybir.dt.float16
U32 = mybir.dt.uint32
ALU = mybir.AluOpType
ACT = mybir.ActivationFunctionType

BATCH, ROWS, COLS, CH = 16, 56, 56, 256
KH, KW = 3, 3
P = 128
HALVES = CH // P
GROUP_CH = CH // 32
EPS = 1e-5
THRESHOLD = 0.7
SPLIT_SCALE = 128.0

QUARTERS = 4
UNITS = BATCH * QUARTERS
UROWS = ROWS // QUARTERS
PAIRS = UROWS // 2
NPOS = PAIRS * COLS
BLOCK = 2 * COLS
BLOCKS = UROWS // 2
BATCHES = ((0, 4), (4, 3))
PCOLS = COLS + 2
TROWS = 4 * PAIRS
BANK = 512

QUAD = 32
QUADS = P // QUAD
PIECE = ROWS * COLS // 2
PIECES = UNITS // 2
XSLOTS = 2
OSLOTS = 2
ZSLOTS = 4
LEAD = 5
FILTER = (1, 2, 0, 3)
FIRST_ROW = (0, 2 * PAIRS, 3 * PAIRS, 1)
ROW_STEP = (2, 1, 1, 2)
TOUT_GAPS = (6, 2)
MEAN_GAP, VAR_GAP = 6, 7
CHAIN = 12


def build(nc, x, w, b, out):
    x_pixels = x.rearrange("n h w c -> (n h w) c").rearrange("(u g p) c -> u p g c", g=PIECE // QUAD, p=QUAD)
    out_units = out.rearrange("n h w c -> (n h w) c").rearrange("(u t p) c -> u p t c", t=BLOCKS, p=BLOCK)
    n_weights = KH * KW * CH * CH
    w_len = n_weights // P
    w_row = w_len // KH

    with ExitStack() as ctx:
        def sb(name, shape, dt=F32):
            return ctx.enter_context(nc.sbuf_tensor(name, shape, dt))

        def ps(name, shape):
            return ctx.enter_context(nc.psum_tensor(name, shape, F32))

        def sem(name):
            return ctx.enter_context(nc.semaphore(name))

        x_in = sb("x_in", [P, XSLOTS, PIECE // QUAD, HALVES, QUAD])
        x_out = sb("x_out", [P, OSLOTS, BLOCKS, CH])
        xT = sb("xT", [P, 2, HALVES, ROWS + 2, COLS])
        U = sb("U", [P, HALVES, TROWS, COLS])
        Z = sb("Z", [P, ZSLOTS, 2, HALVES, TROWS, PCOLS], F16)
        results = sb("results", [P, 7 * NPOS])
        Y = results[:, 0:4 * NPOS].rearrange("p (c n) -> p c n", c=2)
        AB = results[:, 4 * NPOS:6 * NPOS].rearrange("p (j n) -> p j n", j=2)
        m1_sb = results[:, 6 * NPOS:7 * NPOS]
        filt = sb("filt", [P, 4, KW, HALVES, 2, P], F16)
        ident = sb("ident", [P, P])
        ones = sb("ones", [P, P])
        group_avg = sb("group_avg", [P, P])
        bias = sb("bias", [P, HALVES])
        parts = sb("parts", [P, 2, HALVES, 2])
        neg_shift = sb("neg_shift", [P, HALVES])
        totals = sb("totals", [P, 2, HALVES])
        off = sb("off", [P, HALVES])
        unread = sb("unread", [P, 2, PIECE], F16)
        ch_stats = sb("ch_stats", [P, HALVES, 2])
        mean = sb("mean", [P, HALVES])
        neg2mean = sb("neg2mean", [P, HALVES])
        dev = sb("dev", [P, HALVES])
        spread = sb("spread", [P, HALVES])
        var = sb("var", [P, HALVES])
        std = sb("std", [P, HALVES])
        inv0 = sb("inv0", [P, HALVES])
        corr = sb("corr", [P, HALVES])
        scale = sb("scale", [P, HALVES])
        w_ter = sb("w_ter", [P, KH, w_row], F16)
        w_sum = sb("w_sum", [P, KH])
        thr = sb("thr", [P, 1])
        neg_thr = sb("neg_thr", [P, 1])
        kept = sb("kept", [P, KH, 2])
        kept_all = sb("kept_all", [P, 2])
        inv_n = sb("inv_n", [P, 1])
        alpha = sb("alpha", [P, 1])

        w_raw = xT[:, 1].rearrange("p h r c -> p (h r c)")[:, 0:w_len].rearrange("p (k n) -> p k n", k=KH)
        w_abs = Z[:, 2:4].rearrange("p s a h r c -> p (s a h r c)")[:, 0:2 * w_len].bitcast(F32).rearrange(
            "p (k n) -> p k n", k=KH)
        w_mark = results[:, 0:w_len // 2].bitcast(F16).rearrange("p (k n) -> p k n", k=KH)

        M1 = ps("M1", [P, BANK])
        M2 = ps("M2", [P, BANK])
        M03 = ps("M03", [P, 2, 2, BANK])
        tout = ps("tout", [P, 2, BANK])
        sums_at = NPOS + 8
        w_totals = M03[:, 1, 1]

        w_loaded = [sem(f"w_loaded{k}") for k in range(KH)]
        b_loaded = sem("b_loaded")
        x_loaded = [sem(f"x_loaded{i}") for i in range(XSLOTS)]
        x_stored = [sem(f"x_stored{i}") for i in range(OSLOTS)]
        consts_made = sem("consts_made")
        pads_made = sem("pads_made")
        w_abs_made = sem("w_abs_made")
        w_sums = sem("w_sums")
        thr_made = sem("thr_made")
        below_made = sem("below_made")
        ter_made = sem("ter_made")
        filt_step = sem("filt_step")
        kept_step = sem("kept_step")
        kept_summed = sem("kept_summed")
        alpha_step = sem("alpha_step")
        x_turned = sem("x_turned")
        x_summed = sem("x_summed")
        shifted = sem("shifted")
        squared = sem("squared")
        ch_stats_ready = sem("ch_stats_ready")
        group_sums = sem("group_sums")
        spread_ready = sem("spread_ready")
        var_read = sem("var_read")
        std_made = sem("std_made")
        stat_step = sem("stat_step")
        u_made = sem("u_made")
        hi_made = sem("hi_made")
        lo_made = sem("lo_made")
        mm_done = sem("mm_done")
        m1_copied = sem("m1_copied")
        ab_made = sem("ab_made")
        y_made = sem("y_made")
        relu_made = sem("relu_made")
        tout_done = sem("tout_done")
        added = sem("added")
        evacuated = sem("evacuated")

        block = ctx.enter_context(nc.Block())

        def present(s, inside):
            if inside:
                return True, True, True, True
            return s + LEAD < UNITS, 0 <= s + 1 < UNITS, 0 <= s < UNITS, s >= 1

        @block.sync
        def _(sp):
            for k in range(KH):
                for q in range(QUADS):
                    for h in range(HALVES):
                        first = QUAD * (HALVES * q + h)
                        sp.dma_start(w_raw[QUAD * q:QUAD * (q + 1), k].rearrange(
                                         "p (b h c) -> p b h c", b=KW, c=CH)[:, :, h],
                                     w[k, :, first:first + QUAD].rearrange("b p c -> p b c")
                                     ).then_inc(w_loaded[k], 16)

            def load(piece, slot):
                for q in range(QUADS):
                    sp.dma_start(x_in[QUAD * q:QUAD * (q + 1), slot].rearrange("p g h c -> p g (h c)"),
                                 x_pixels[piece, :, :, 2 * QUAD * q:2 * QUAD * (q + 1)]).then_inc(x_loaded[slot], 16)

            def store(s, j):
                sp.wait_ge(evacuated, 4 * s + 4)
                sp.dma_start(out_units[s], x_out[0:BLOCK, j % OSLOTS]).then_inc(x_stored[j % OSLOTS], 16)

            for piece in range(LEAD - 1):
                if piece >= XSLOTS:
                    sp.wait_ge(x_turned, 2 * (piece - XSLOTS) + 2)
                load(piece, piece % XSLOTS)
            with sp.Fori(0, (UNITS - 8) // 8) as k:
                for j in range(1, 9):
                    if j % 2:
                        sp.wait_ge(x_turned, k * 8 + (j + 5))
                        load(k * 4 + (j + 7) // 2, (j + 7) // 2 % XSLOTS)
                    store(k * 8 + (j - 1), j - 1)
            for s in range(UNITS - 8, UNITS):
                store(s, s)
            for slot in range(OSLOTS):
                sp.wait_ge(x_stored[slot], 16 * UNITS // OSLOTS)

        @block.gpsimd
        def _(pool):
            for q in range(QUADS):
                pool.dma_start(bias[QUAD * q:QUAD * (q + 1), :],
                               b[2 * QUAD * q:2 * QUAD * (q + 1)].rearrange("(h p) -> p h", p=QUAD),
                               allow_slow_non_contiguous=True).then_inc(b_loaded, 16)
            pool.memset(ones[:, :], 1.0).then_inc(consts_made, 1)
            pool.memset(ident[:, :], 0.0).then_inc(consts_made, 1)
            pool.memset(group_avg[:, :], 1.0 / GROUP_CH).then_inc(consts_made, 1)
            pool.memset(Z[:, 0:2, :, :, :, 0:PCOLS:PCOLS - 1].rearrange("p s a h r c -> p (s a h r) c"),
                        0.0).then_inc(pads_made, 1)
            pool.wait_ge(consts_made, 3)
            pool.affine_select(out=ident[:, :], in_=ident[:, :], compare_op=ALU.not_equal, fill=1.0, base=0,
                               pattern=[[-1, P]], channel_multiplier=1).then_inc(consts_made, 1)
            g_view = group_avg[:, :].rearrange("p (g e) -> p g e", e=GROUP_CH)
            pool.affine_select(out=g_view, in_=g_view, compare_op=ALU.is_ge, fill=0.0, base=0,
                               pattern=[[-GROUP_CH, P // GROUP_CH], [0, GROUP_CH]],
                               channel_multiplier=1).then_inc(consts_made, 1)
            pool.wait_ge(consts_made, 5)
            pool.affine_select(out=g_view, in_=g_view, compare_op=ALU.is_ge, fill=0.0, base=GROUP_CH - 1,
                               pattern=[[GROUP_CH, P // GROUP_CH], [0, GROUP_CH]],
                               channel_multiplier=-1).then_inc(consts_made, 1)
            pool.wait_ge(thr_made, 1)
            for k in range(KH):
                pool.tensor_scalar(w_mark[:, k], w_abs[:, k], thr[:, :], None, ALU.is_gt).then_inc(kept_step, 1)
                pool.wait_ge(kept_step, 2 * k + 1)
                pool.tensor_tensor(w_abs[:, k], w_abs[:, k], w_mark[:, k], ALU.mult).then_inc(kept_step, 1)
            pool.wait_ge(kept_summed, 2 * KH)
            pool.memset(Z[:, 2:4, :, :, :, 0:PCOLS:PCOLS - 1].rearrange("p s a h r c -> p (s a h r) c"),
                        0.0).then_inc(pads_made, 1)

        @block.scalar
        def _(act):
            for k in range(KH):
                act.wait_ge(w_loaded[k], 16 * QUADS * HALVES)
                act.activation(w_abs[:, k], w_raw[:, k], ACT.Abs, accum_out=w_sum[:, k:k + 1]
                               ).then_inc(w_abs_made, 1)

            def sum_kept(rows):
                for k in rows:
                    act.wait_ge(kept_step, 2 * k + 2)
                    act.activation(w_mark[:, k], w_mark[:, k], ACT.Copy, accum_out=kept[:, k, 0:1]
                                   ).then_inc(kept_summed, 1)
                    act.activation(w_abs[:, k], w_abs[:, k], ACT.Copy, accum_out=kept[:, k, 1:2]
                                   ).then_inc(kept_summed, 1)

            def measure(u, j, m):
                t, par = j % QUARTERS, j // QUARTERS % 2
                piece, half = t // 2, t % 2
                rows = xT[:, par, half, 1 + piece * ROWS // 2:1 + (piece + 1) * ROWS // 2, :].rearrange(
                    "p r c -> p (r c)")
                if t == 0 and not (type(u) is int and u == 0):
                    act.wait_ge(ch_stats_ready, m)
                act.wait_ge(x_turned, u + 1)
                if not (type(u) is int and u == 0):
                    act.wait_ge(x_summed, u)
                act.activation(unread[:, 0], rows, ACT.Copy, accum_out=parts[:, 0, half, piece:piece + 1]
                               ).then_inc(x_summed, 1)
                if piece == 0:
                    act.wait_ge(x_summed, u + 1)
                    act.mul(neg_shift[:, half:half + 1], parts[:, 0, half, 0:1], -1.0 / PIECE
                            ).then_inc(shifted, 1)
                    act.wait_ge(shifted, 2 * m + 1 + half)
                if not (type(u) is int and u == 0):
                    act.wait_ge(squared, u)
                act.activation(unread[:, 1], rows, ACT.Square, bias=neg_shift[:, half:half + 1],
                               accum_out=parts[:, 1, half, piece:piece + 1]).then_inc(squared, 1)

            def evacuate(s, j, c):
                for n, (first, count) in enumerate(BATCHES):
                    act.wait_ge(tout_done, 4 * s + 2 * c + n + 1)
                    if c == 0 and n == 0 and not (type(s) is int and s < OSLOTS):
                        act.wait_ge(x_stored[j % OSLOTS], 8 * s - 8 * (j % OSLOTS))
                    act.activation(x_out[0:BLOCK, j % OSLOTS, first:first + count].rearrange(
                                       "p t (q h e) -> p t q h e", q=QUADS, e=QUAD)[:, :, :, c],
                                   tout[0:BLOCK, n, 0:count * P].rearrange("p (t q e) -> p t q e", q=QUADS, e=QUAD),
                                   ACT.Copy).then_inc(evacuated, 1)

            def high(v, j, half):
                slot = j % ZSLOTS
                act.wait_ge(u_made, 2 * v + half + 1)
                if half == 0:
                    if type(v) is int and v < 2:
                        act.wait_ge(pads_made, 1)
                    else:
                        act.wait_ge(pads_made, 2)
                        act.wait_ge(mm_done, 8 * v - 15)
                act.activation(Z[:, slot, 0, half, :, 1:COLS + 1], U[:, half], ACT.Copy,
                               scale=scale[:, half:half + 1]).then_inc(hi_made, 1)

            def copy_m1(s, c):
                act.wait_ge(mm_done, 8 * s + 4 * c + 1)
                if not (type(s) is int and 2 * s + c < 1):
                    act.wait_ge(ab_made, 2 * s + c)
                act.activation(m1_sb[:, :], M1[:, 0:NPOS], ACT.Copy).then_inc(m1_copied, 1)

            def relu(s, c):
                act.wait_ge(y_made, 2 * s + c + 1)
                act.activation(Y[:, c], Y[:, c], ACT.Relu, bias=bias[:, c:c + 1],
                               scale=alpha[:, :]).then_inc(relu_made, 1)

            def step(s, j, image, inside=False):
                do_tin, do_tr, do_mm, do_end = present(s, inside)
                fixed = type(s) is int
                if do_end:
                    relu(s - 1, 1)
                if do_tr and (j + 1) % QUARTERS == 0:
                    act.wait_ge(var_read, image(j + 1) + 1)
                    act.activation(std[:, :], var[:, :], ACT.Sqrt).then_inc(std_made, 1)
                if do_mm:
                    copy_m1(s, 0)
                if fixed and s == -3:
                    sum_kept(range(KH - 1))
                if do_tr:
                    high(s + 1, j + 1, 0)
                if fixed and s == -1:
                    high(0, 0, 1)
                    sum_kept(range(KH - 1, KH))
                if do_end:
                    evacuate(s - 1, j - 1, 1)
                if do_tin:
                    measure(s + LEAD, j + LEAD, image(j + LEAD))
                if do_mm:
                    if fixed and s == 0:
                        act.wait_ge(b_loaded, 16 * QUADS)
                        act.wait_ge(alpha_step, 3)
                    relu(s, 0)
                    copy_m1(s, 1)
                if do_tr and not (fixed and s == -1):
                    high(s + 1, j + 1, 1)
                if do_mm:
                    evacuate(s, j, 0)

            for s in range(-LEAD, 1):
                step(s, s, lambda n: n // QUARTERS)
            with act.Fori(0, (UNITS - 8) // 8) as k:
                for j in range(1, 9):
                    step(k * 8 + j, j, lambda n: k * 2 + n // QUARTERS, True)
            for s in range(UNITS - 7, UNITS + 1):
                step(s, s, lambda n: n // QUARTERS)

        @block.vector
        def _(dve):
            def make_threshold():
                dve.wait_ge(w_sums, 1)
                dve.tensor_scalar(thr[:, :], w_totals[:, 0:1], 1.0 / n_weights, THRESHOLD, ALU.mult, ALU.mult
                                  ).then_inc(thr_made, 1)
                dve.wait_ge(thr_made, 1)
                dve.tensor_scalar(neg_thr[:, :], thr[:, :], -1.0, None, ALU.mult).then_inc(thr_made, 1)

            def make_filters():
                dve.wait_ge(thr_made, 2)
                flat = [filt[:, i].rearrange("p b h c e -> p (b h c e)") for i in range(4)]
                for k in range(KH):
                    dve.tensor_scalar(flat[k], w_raw[:, k], neg_thr[:, :], None, ALU.is_le).then_inc(below_made, 1)
                for k in range(KH):
                    dve.wait_ge(below_made, k + 1)
                    dve.scalar_tensor_tensor(w_ter[:, k], w_raw[:, k], thr[:, :], flat[k],
                                             ALU.is_ge, ALU.subtract).then_inc(ter_made, 1)
                dve.wait_ge(ter_made, KH)
                dve.tensor_tensor(flat[3], w_ter[:, 0], w_ter[:, 2], ALU.add).then_inc(filt_step, 1)
                dve.wait_ge(filt_step, 1)

                def of_half(row, c):
                    return row.rearrange("p (n q c e) -> p n q c e", q=QUADS, c=2, e=QUAD)[:, :, :, c]

                def dst(i, c):
                    return filt[:, i, :, :, c].rearrange("p b h (q e) -> p (b h) q e", e=QUAD)

                for c in range(2):
                    ins = dve.tensor_tensor(dst(1, c), of_half(flat[3], c), of_half(w_ter[:, 1], c), ALU.add)
                ins.then_inc(filt_step, 1)
                for c in range(2):
                    ins = dve.tensor_tensor(dst(2, c), of_half(flat[3], c), of_half(w_ter[:, 1], c), ALU.subtract)
                ins.then_inc(filt_step, 1)
                for c in range(2):
                    ins = dve.tensor_scalar(dst(0, c), of_half(w_ter[:, 0], c), -2.0, None, ALU.mult)
                ins.then_inc(filt_step, 1)
                dve.wait_ge(filt_step, 3)
                for c in range(2):
                    ins = dve.tensor_scalar(dst(3, c), of_half(w_ter[:, 2], c), 2.0, None, ALU.mult)
                ins.then_inc(filt_step, 1)

            def make_alpha():
                dve.wait_ge(w_sums, 2)
                dve.tensor_copy(kept_all[:, :], w_totals[:, 2:4]).then_inc(alpha_step, 1)
                dve.wait_ge(alpha_step, 1)
                dve.reciprocal(inv_n[:, :], kept_all[:, 0:1]).then_inc(alpha_step, 1)
                dve.wait_ge(alpha_step, 2)
                dve.scalar_tensor_tensor(alpha[:, :], kept_all[:, 1:2], 0.5 / SPLIT_SCALE, inv_n[:, :],
                                         ALU.mult, ALU.mult).then_inc(alpha_step, 1)

            make_threshold()
            make_filters()

            def turn(u, j):
                t, par = j % QUARTERS, j // QUARTERS % 2
                piece, half, slot = t // 2, t % 2, j // 2 % XSLOTS
                if type(u) is int:
                    loads = u // 2 // XSLOTS + 1
                else:
                    loads = k_of[0] * (8 // 2 // XSLOTS) + (j // 2 // XSLOTS + 1)
                dve.wait_ge(x_loaded[slot], loads * (16 * QUADS))
                rows = xT[:, par, half, 1 + piece * ROWS // 2:1 + (piece + 1) * ROWS // 2, :]
                dve.transpose(rows.rearrange("p r c -> p (r c)").rearrange("p (g e) -> p g e", e=QUAD).bitcast(U32),
                              x_in[:, slot, :, half].bitcast(U32)).then_inc(x_turned, 1)

            k_of = [None]

            def channel_stats(m):
                at = m * CHAIN
                n = 1.0 / (ROWS * COLS)
                dve.reduce_sum(totals[:, :, :], parts[:, :, :, :], mybir.AxisListType.X).then_inc(stat_step, 1)
                dve.wait_ge(stat_step, at + 1)
                dve.tensor_scalar(ch_stats[:, :, 0], totals[:, 0], n, None, ALU.mult).then_inc(stat_step, 1)
                dve.wait_ge(stat_step, at + 2)
                dve.tensor_tensor(off[:, :], ch_stats[:, :, 0], neg_shift[:, :], ALU.add).then_inc(stat_step, 1)
                dve.wait_ge(stat_step, at + 3)
                dve.tensor_tensor(off[:, :], off[:, :], off[:, :], ALU.mult).then_inc(stat_step, 1)
                dve.wait_ge(stat_step, at + 4)
                dve.scalar_tensor_tensor(ch_stats[:, :, 1], totals[:, 1], n, off[:, :], ALU.mult, ALU.subtract
                                         ).then_inc(ch_stats_ready, 1)

            def group_mean(m):
                at = m * CHAIN
                dve.wait_ge(group_sums, 2 * m + 1)
                dve.tensor_copy(mean[:, :], M2[:, sums_at:sums_at + HALVES]).then_inc(stat_step, 1)
                dve.wait_ge(stat_step, at + 5)
                dve.tensor_tensor(dev[:, :], ch_stats[:, :, 0], mean[:, :], ALU.subtract).then_inc(stat_step, 1)
                dve.wait_ge(stat_step, at + 6)
                dve.tensor_tensor(spread[:, :], dev[:, :], dev[:, :], ALU.mult).then_inc(stat_step, 1)
                dve.tensor_scalar(neg2mean[:, :], mean[:, :], -2.0, None, ALU.mult)
                dve.wait_ge(stat_step, at + 7)
                dve.tensor_tensor(spread[:, :], spread[:, :], ch_stats[:, :, 1], ALU.add).then_inc(spread_ready, 1)

            def group_var(m):
                dve.wait_ge(group_sums, 2 * m + 2)
                dve.tensor_scalar(var[:, :], M2[:, sums_at + 8:sums_at + 8 + HALVES], EPS, None, ALU.add).then_inc(var_read, 1)

            def group_scale(m, par):
                at = m * CHAIN
                for half in range(HALVES):
                    dve.tensor_scalar(xT[:, par, half, 0:ROWS + 2:ROWS + 1, :],
                                      ones[:, 0:2 * COLS].rearrange("p (r c) -> p r c", r=2),
                                      mean[:, half:half + 1], None, ALU.mult)
                dve.wait_ge(std_made, m + 1)
                dve.reciprocal(inv0[:, :], std[:, :]).then_inc(stat_step, 1)
                dve.wait_ge(stat_step, at + 8)
                dve.tensor_tensor(corr[:, :], inv0[:, :], inv0[:, :], ALU.mult).then_inc(stat_step, 1)
                dve.wait_ge(stat_step, at + 9)
                dve.tensor_tensor(corr[:, :], corr[:, :], var[:, :], ALU.mult).then_inc(stat_step, 1)
                dve.wait_ge(stat_step, at + 10)
                dve.tensor_scalar(corr[:, :], corr[:, :], -0.5 * SPLIT_SCALE, 1.5 * SPLIT_SCALE,
                                  ALU.mult, ALU.add).then_inc(stat_step, 1)
                dve.wait_ge(stat_step, at + 11)
                dve.tensor_tensor(scale[:, :], corr[:, :], inv0[:, :], ALU.mult).then_inc(stat_step, 1)
                dve.wait_ge(stat_step, at + 12)

            def transform(v, j, half):
                if not (type(v) is int and v == 0):
                    dve.wait_ge(lo_made, 2 * v + half - 1)
                t, par = j % QUARTERS, j // QUARTERS % 2
                row = UROWS * t
                src, dst = xT[:, par, half], U[:, half]
                dve.tensor_tensor(dst[:, 0:UROWS].rearrange("p r c -> p (r c)"),
                                  src[:, row + 2:row + 2 + UROWS].rearrange("p r c -> p (r c)"),
                                  src[:, row:row + UROWS].rearrange("p r c -> p (r c)"), ALU.subtract)
                even, odd = src[:, row + 1:row + 1 + UROWS:2], src[:, row + 2:row + 2 + UROWS:2]
                dve.scalar_tensor_tensor(dst[:, UROWS:UROWS + PAIRS], even, neg2mean[:, half:half + 1], odd,
                                         ALU.add, ALU.add)
                dve.tensor_tensor(dst[:, UROWS + PAIRS:TROWS], odd, even, ALU.subtract).then_inc(u_made, 1)

            def low(v, j, half):
                slot = j % ZSLOTS
                dve.wait_ge(hi_made, 2 * v + half + 1)
                dve.scalar_tensor_tensor(Z[:, slot, 1, half, :, 1:COLS + 1], U[:, half],
                                         scale[:, half:half + 1], Z[:, slot, 0, half, :, 1:COLS + 1],
                                         ALU.mult, ALU.subtract).then_inc(lo_made, 1)

            def sum_and_difference(s, c):
                dve.wait_ge(m1_copied, 2 * s + c + 1)
                if type(s) is int and s == 0 and c == 0:
                    dve.wait_ge(kept_summed, 2 * KH)
                dve.wait_ge(mm_done, 8 * s + 4 * c + 2)
                dve.tensor_tensor(AB[:, 0], m1_sb[:, :], M2[:, 0:NPOS], ALU.add)
                dve.tensor_tensor(AB[:, 1], m1_sb[:, :], M2[:, 0:NPOS], ALU.subtract).then_inc(ab_made, 1)

            def join(s, c, first=False):
                dve.wait_ge(mm_done, 8 * s + 4 * c + 4)
                dve.wait_ge(ab_made, 2 * s + c + 1)
                if c == 1:
                    dve.wait_ge(tout_done, 4 * s + 1)
                elif not first:
                    dve.wait_ge(tout_done, 4 * s - 2)
                dve.tensor_tensor(Y[:, c].rearrange("p (r j c) -> p j r c", j=2, c=COLS),
                                  AB[:, :].rearrange("p j (r c) -> p j r c", c=COLS),
                                  M03[:, c, :, 0:NPOS].rearrange("p j (r c) -> p j r c", c=COLS),
                                  ALU.add).then_inc(y_made, 1)

            def add_residual(s, j, c):
                dve.wait_ge(relu_made, 2 * s + c + 1)
                row = 1 + UROWS * (j % QUARTERS)
                dve.tensor_tensor(Y[:, c], Y[:, c],
                                  xT[:, j // QUARTERS % 2, c, row:row + UROWS].rearrange("p r c -> p (r c)"),
                                  ALU.add).then_inc(added, 1)

            def step(s, j, image, inside=False):
                do_tin, do_tr, do_mm, do_end = present(s, inside)
                fixed = type(s) is int
                u, v = s + LEAD, s + 1
                last_quarter = do_tin and (j + LEAD) % QUARTERS == QUARTERS - 1
                if do_end:
                    join(s - 1, 1)
                if do_tr and (j + 1) % QUARTERS == 0:
                    m = image(j + 1)
                    group_var(m)
                    group_scale(m, (j + 1) // QUARTERS % 2)
                if do_tr:
                    transform(v, j + 1, 0)
                if do_end:
                    add_residual(s - 1, j - 1, 1)
                if fixed and s == -1:
                    transform(0, 0, 1)
                    low(0, 0, 0)
                    low(0, 0, 1)
                    do_tr = False
                if do_tin:
                    turn(u, j + LEAD)
                if do_mm:
                    sum_and_difference(s, 0)
                if do_tr:
                    low(v, j + 1, 0)
                if fixed and s == 0:
                    make_alpha()
                if do_mm:
                    join(s, 0, first=fixed and s == 0)
                if do_tr:
                    transform(v, j + 1, 1)
                if do_mm:
                    add_residual(s, j, 0)
                    sum_and_difference(s, 1)
                if last_quarter:
                    dve.wait_ge(squared, u + 1)
                    channel_stats(image(j + 2))
                if do_tr:
                    low(v, j + 1, 1)
                if last_quarter:
                    group_mean(image(j + 2))

            for s in range(-LEAD, 1):
                step(s, s, lambda n: n // QUARTERS)
            with dve.Fori(0, (UNITS - 8) // 8) as k:
                k_of[0] = k
                for j in range(1, 9):
                    step(k * 8 + j, j, lambda n: k * 2 + n // QUARTERS, True)
            for s in range(UNITS - 7, UNITS + 1):
                step(s, s, lambda n: n // QUARTERS)

        @block.tensor
        def _(pe):
            pe.wait_ge(consts_made, 6)

            def sum_sizes():
                for k in range(KH):
                    pe.wait_ge(w_abs_made, k + 1)
                    ins = pe.matmul(w_totals[:, 0:1], ones[:, :], w_sum[:, k:k + 1],
                                    start=k == 0, stop=k == KH - 1)
                ins.then_inc(w_sums, 1)

            sum_sizes()

            def transpose_y(s, c):
                pe.wait_ge(added, 2 * s + c + 1)
                for n, (first, count) in enumerate(BATCHES):
                    if not (type(s) is int and s == 0 and c == 0):
                        pe.wait_ge(evacuated, 4 * s + 2 * c + n - 1)
                    for i in range(count):
                        ins = pe.transpose(tout[0:BLOCK, n, i * P:(i + 1) * P],
                                           Y[:, c, (first + i) * BLOCK:(first + i + 1) * BLOCK], ident[:, :])
                    ins.then_inc(tout_done, 1)

            def product(s, j, c, i):
                past = 2 * s + c
                if i == 1:
                    target = M1[:, 0:NPOS]
                    free, count = m1_copied, past
                elif i == 2:
                    target = M2[:, 0:NPOS]
                    free, count = ab_made, past
                else:
                    target = M03[:, c, i // 3, 0:NPOS]
                    free, count = y_made, past - 1
                if i != 3 and not (type(count) is int and count < 1):
                    pe.wait_ge(free, count)
                n = 0
                for kw in range(KW):
                    for half in range(HALVES):
                        for part in range(2):
                            first, row_step = FIRST_ROW[i], ROW_STEP[i]
                            ins = pe.matmul(target, filt[:, i, kw, half, c],
                                            Z[:, j % ZSLOTS, part, half,
                                              first:first + row_step * (PAIRS - 1) + 1:row_step, kw:kw + COLS],
                                            start=n == 0, stop=n == 2 * KW * HALVES - 1)
                            n += 1
                ins.then_inc(mm_done, 1)

            def step(s, j, image, inside=False):
                do_tin, do_tr, do_mm, do_end = present(s, inside)
                fixed = type(s) is int
                last_quarter = do_tin and (j + LEAD) % QUARTERS == QUARTERS - 1
                if do_mm:
                    pe.wait_ge(hi_made, 2 * s + 2)
                    pe.wait_ge(lo_made, 2 * s + 2)
                for g in range(8):
                    if fixed and s == 0 and g < 4:
                        pe.wait_ge(filt_step, g + 2)
                    if do_tr and g == 1 and (j + 1) % QUARTERS == 0:
                        pe.wait_ge(var_read, image(j + 1) + 1)
                    if do_mm:
                        product(s, j, g // 4, FILTER[g % 4])
                    if fixed and s == 0 and g == 4:
                        pe.wait_ge(kept_summed, 2 * KH)
                        for k in range(KH):
                            ins = pe.matmul(w_totals[:, 2:4], ones[:, :], kept[:, k], start=k == 0, stop=k == KH - 1)
                        ins.then_inc(w_sums, 1)
                    if do_end and g == TOUT_GAPS[1]:
                        transpose_y(s - 1, 1)
                    if do_mm and g == TOUT_GAPS[0]:
                        transpose_y(s, 0)
                    if last_quarter and g == MEAN_GAP:
                        pe.wait_ge(ch_stats_ready, image(j + 2) + 1)
                        if do_mm:
                            pe.wait_ge(ab_made, 2 * s + 2)
                        pe.matmul(M2[:, sums_at:sums_at + HALVES], group_avg[:, :], ch_stats[:, :, 0],
                                  start=True, stop=True).then_inc(group_sums, 1)
                    if last_quarter and g == VAR_GAP:
                        pe.wait_ge(spread_ready, image(j + 2) + 1)
                        pe.matmul(M2[:, sums_at + 8:sums_at + 8 + HALVES], group_avg[:, :], spread[:, :],
                                  start=True, stop=True).then_inc(group_sums, 1)

            for s in range(-LEAD, 1):
                step(s, s, lambda n: n // QUARTERS)
            with pe.Fori(0, (UNITS - 8) // 8) as k:
                for j in range(1, 9):
                    step(k * 8 + j, j, lambda n: k * 2 + n // QUARTERS, True)
            for s in range(UNITS - 7, UNITS + 1):
                step(s, s, lambda n: n // QUARTERS)


def kernel(x, L0_conv_W, L0_conv_b):
    import numpy as _np
    import concourse.bacc as _bacc
    from concourse.bass_utils import run_bass_kernel_spmd as _run

    nc = _bacc.Bacc("TRN2", target_bir_lowering=False, num_devices=1)
    arrays, args = {}, []
    for name, a in (("x", x), ("w", L0_conv_W), ("b", L0_conv_b)):
        a = _np.ascontiguousarray(a)
        arrays[name] = a
        args.append(nc.dram_tensor(name, a.shape, mybir.dt.from_np(a.dtype), kind="ExternalInput").ap())
    args.append(nc.dram_tensor("out", arrays["x"].shape, F32, kind="ExternalOutput").ap())
    build(nc, *args)
    return _run(nc, [arrays], core_ids=[0]).results[0]["out"]
```

```python
from contextlib import ExitStack

import concourse.bass as bass
from concourse import mybir

F32 = mybir.dt.float32
F16 = mybir.dt.float16
U32 = mybir.dt.uint32
ALU = mybir.AluOpType
ACT = mybir.ActivationFunctionType

BATCH, ROWS, COLS, CH = 16, 56, 56, 256
KH, KW = 3, 3
P = 128
HALVES = CH // P
GROUP_CH = CH // 32
EPS = 1e-5
THRESHOLD = 0.7
SPLIT_SCALE = 128.0

QUARTERS = 4
UNITS = BATCH * QUARTERS
UROWS = ROWS // QUARTERS
PAIRS = UROWS // 2
NPOS = PAIRS * COLS
PCOLS = COLS + 2
TROWS = 4 * PAIRS
BANK = 512

QUAD = 32
QUADS = P // QUAD
PIECE = ROWS * COLS // 2
GROUPS = PIECE // QUAD
FIRST_GROUP = (0, 24)
N_GROUPS = (24, 25)
XSLOTS = 2
OSLOTS = 4
ZSLOTS = 2
LEAD = 5
FILTER = (1, 2, 0, 3)
FIRST_ROW = (0, 2 * PAIRS, 3 * PAIRS, 1)
ROW_STEP = (2, 1, 1, 2)
MEAN_GAP, VAR_GAP = 5, 7
CHAIN = 12


def build(nc, x, w, b, out):
    x_pixels = x.rearrange("n h w c -> (n h w) c").rearrange("(u g p) c -> u p g c", g=GROUPS, p=QUAD)
    out_pixels = out.rearrange("n h w c -> (n h w) c").rearrange("(u g p) c -> u p g c", g=GROUPS, p=QUAD)
    n_weights = KH * KW * CH * CH
    w_len = n_weights // P
    w_row = w_len // KH

    with ExitStack() as ctx:
        def sb(name, shape, dt=F32):
            return ctx.enter_context(nc.sbuf_tensor(name, shape, dt))

        def ps(name, shape):
            return ctx.enter_context(nc.psum_tensor(name, shape, F32))

        def sem(name):
            return ctx.enter_context(nc.semaphore(name))

        x_in = sb("x_in", [P, XSLOTS, GROUPS, HALVES, QUAD])
        staging = sb("staging", [P, w_len + w_len // 2])
        xT = sb("xT", [P, 2, HALVES, ROWS + 2, COLS])
        U = sb("U", [P, HALVES, TROWS, COLS])
        Z = sb("Z", [P, ZSLOTS, 2, HALVES, TROWS, PCOLS], F16)
        Y = sb("Y", [P, 2, PIECE])
        AB = sb("AB", [P, 2, NPOS])
        m1_sb = sb("m1_sb", [P, NPOS])
        filt = sb("filt", [P, 4, KW, HALVES, 2, P], F16)
        ones = sb("ones", [P, P])
        group_avg = sb("group_avg", [P, P])
        bias = sb("bias", [P, HALVES])
        parts = sb("parts", [P, 2, HALVES, 2])
        neg_shift = sb("neg_shift", [P, HALVES])
        totals = sb("totals", [P, 2, HALVES])
        off = sb("off", [P, HALVES])
        unread = sb("unread", [P, PIECE])
        ch_stats = sb("ch_stats", [P, HALVES, 2])
        mean = sb("mean", [P, HALVES])
        neg2mean = sb("neg2mean", [P, HALVES])
        dev = sb("dev", [P, HALVES])
        spread = sb("spread", [P, HALVES])
        var = sb("var", [P, HALVES])
        std = sb("std", [P, HALVES])
        inv0 = sb("inv0", [P, HALVES])
        corr = sb("corr", [P, HALVES])
        scale = sb("scale", [P, HALVES])
        w_ter = sb("w_ter", [P, KH, w_row], F16)
        w_sum = sb("w_sum", [P, KH])
        thr = sb("thr", [P, 1])
        neg_thr = sb("neg_thr", [P, 1])
        kept = sb("kept", [P, KH, 2])
        kept_all = sb("kept_all", [P, 2])
        inv_n = sb("inv_n", [P, 1])
        alpha = sb("alpha", [P, 1])

        slot_len = N_GROUPS[1] * HALVES * QUAD
        x_out = staging[:, 0:OSLOTS * slot_len].rearrange("p (o g h c) -> p o g h c", o=OSLOTS, h=HALVES, c=QUAD)

        w_raw = xT[:, 1].rearrange("p h r c -> p (h r c)")[:, 0:w_len].rearrange("p (k n) -> p k n", k=KH)
        w_abs = staging[:, 0:w_len].rearrange("p (k n) -> p k n", k=KH)
        w_mark = staging[:, w_len:].bitcast(F16).rearrange("p (k n) -> p k n", k=KH)

        M1 = ps("M1", [P, 2, BANK])
        M2 = ps("M2", [P, 2, BANK])
        M03 = ps("M03", [P, 2, 2, BANK])
        sums_at = NPOS + 8
        w_totals = M03[:, 1, 1]

        w_loaded = [sem(f"w_loaded{k}") for k in range(KH)]
        b_loaded = sem("b_loaded")
        x_loaded = [sem(f"x_loaded{i}") for i in range(XSLOTS)]
        out_free = [sem(f"out_free{i}") for i in range(OSLOTS)]
        consts_made = sem("consts_made")
        pads_made = sem("pads_made")
        w_abs_made = sem("w_abs_made")
        w_sums = sem("w_sums")
        thr_made = sem("thr_made")
        below_made = sem("below_made")
        ter_made = sem("ter_made")
        filt_step = sem("filt_step")
        kept_step = sem("kept_step")
        kept_summed = sem("kept_summed")
        alpha_step = sem("alpha_step")
        x_turned = sem("x_turned")
        x_summed = sem("x_summed")
        shifted = sem("shifted")
        squared = sem("squared")
        ch_stats_ready = sem("ch_stats_ready")
        group_sums = sem("group_sums")
        spread_ready = sem("spread_ready")
        var_read = sem("var_read")
        std_made = sem("std_made")
        stat_step = sem("stat_step")
        edges_made = sem("edges_made")
        u_made = sem("u_made")
        hi_made = sem("hi_made")
        lo_made = sem("lo_made")
        mm_done = sem("mm_done")
        m1_copied = sem("m1_copied")
        ab_made = sem("ab_made")
        y_made = sem("y_made")
        relu_made = sem("relu_made")
        added = sem("added")
        turned_back = sem("turned_back")

        block = ctx.enter_context(nc.Block())

        def present(s, inside):
            if inside:
                return True, True, True, True
            return s + LEAD < UNITS, 0 <= s + 1 < UNITS, 0 <= s < UNITS, s >= 1

        @block.sync
        def _(sp):
            def load(piece, slot):
                for q in range(QUADS):
                    sp.dma_start(x_in[QUAD * q:QUAD * (q + 1), slot].rearrange("p g h c -> p g (h c)"),
                                 x_pixels[piece, :, :, 2 * QUAD * q:2 * QUAD * (q + 1)]).then_inc(x_loaded[slot], 16)

            def store(s, piece, j):
                odd, slot = j % 2, j % OSLOTS
                sp.wait_ge(turned_back, 2 * s + 2)
                for q in range(QUADS):
                    sp.dma_start(out_pixels[piece, :, FIRST_GROUP[odd]:FIRST_GROUP[odd] + N_GROUPS[odd],
                                            2 * QUAD * q:2 * QUAD * (q + 1)],
                                 x_out[QUAD * q:QUAD * (q + 1), slot, 0:N_GROUPS[odd]].rearrange(
                                     "p g h c -> p g (h c)")).then_inc(out_free[slot], 16)

            load(0, 0)
            for k in range(KH):
                for q in range(QUADS):
                    for h in range(HALVES):
                        first = QUAD * (HALVES * q + h)
                        sp.dma_start(w_raw[QUAD * q:QUAD * (q + 1), k].rearrange(
                                         "p (b h c) -> p b h c", b=KW, c=CH)[:, :, h],
                                     w[k, :, first:first + QUAD].rearrange("b p c -> p b c")
                                     ).then_inc(w_loaded[k], 16)
            for piece in range(1, LEAD - 1):
                if piece >= XSLOTS:
                    sp.wait_ge(x_turned, 2 * (piece - XSLOTS) + 2)
                load(piece, piece % XSLOTS)
            with sp.Fori(0, (UNITS - 8) // 8) as k:
                for j in range(1, 9):
                    if j % 2:
                        sp.wait_ge(x_turned, k * 8 + (j + 5))
                        load(k * 4 + (j + 7) // 2, (j + 7) // 2 % XSLOTS)
                    store(k * 8 + (j - 1), k * 4 + (j - 1) // 2, j - 1)
            for s in range(UNITS - 8, UNITS):
                store(s, s // 2, s)
            for slot in range(OSLOTS):
                sp.wait_ge(out_free[slot], 16 * QUADS * UNITS // OSLOTS + 1)

        @block.gpsimd
        def _(pool):
            for q in range(QUADS):
                pool.dma_start(bias[QUAD * q:QUAD * (q + 1), :],
                               b[2 * QUAD * q:2 * QUAD * (q + 1)].rearrange("(h p) -> p h", p=QUAD),
                               allow_slow_non_contiguous=True).then_inc(b_loaded, 16)
            pool.memset(ones[:, :], 1.0).then_inc(consts_made, 1)
            pool.memset(group_avg[:, :], 1.0 / GROUP_CH).then_inc(consts_made, 1)
            pool.memset(Z[:, :, :, :, :, 0:PCOLS:PCOLS - 1].rearrange("p s a h r c -> p (s a h r) c"),
                        0.0).then_inc(pads_made, 1)
            pool.wait_ge(consts_made, 2)
            g_view = group_avg[:, :].rearrange("p (g e) -> p g e", e=GROUP_CH)
            pool.affine_select(out=g_view, in_=g_view, compare_op=ALU.is_ge, fill=0.0, base=0,
                               pattern=[[-GROUP_CH, P // GROUP_CH], [0, GROUP_CH]],
                               channel_multiplier=1).then_inc(consts_made, 1)
            pool.wait_ge(consts_made, 3)
            pool.affine_select(out=g_view, in_=g_view, compare_op=ALU.is_ge, fill=0.0, base=GROUP_CH - 1,
                               pattern=[[GROUP_CH, P // GROUP_CH], [0, GROUP_CH]],
                               channel_multiplier=-1).then_inc(consts_made, 1)
            pool.wait_ge(thr_made, 1)
            for k in range(KH):
                pool.tensor_scalar(w_mark[:, k], w_abs[:, k], thr[:, :], None, ALU.is_gt).then_inc(kept_step, 1)
                pool.wait_ge(kept_step, 2 * k + 1)
                pool.tensor_tensor(w_abs[:, k], w_abs[:, k], w_mark[:, k], ALU.mult).then_inc(kept_step, 1)
            pool.wait_ge(kept_summed, 2 * KH)
            for slot in range(OSLOTS):
                pool.memset(x_out[:, slot, 0, 0, 0:1], 0.0).then_inc(out_free[slot], 1)

            def add_residual(s, j, c):
                pool.wait_ge(relu_made, 2 * s + c + 1)
                row, at = 1 + UROWS * (j % QUARTERS), j % 2 * 2 * NPOS
                y = Y[:, c, at:at + 2 * NPOS]
                pool.tensor_tensor(y, y, xT[:, j // QUARTERS % 2, c, row:row + UROWS].rearrange("p r c -> p (r c)"),
                                   ALU.add).then_inc(added, 1)

            add_residual(0, 0, 0)
            with pool.Fori(0, (UNITS - 8) // 8) as k:
                for j in range(1, 9):
                    add_residual(k * 8 + (j - 1), j - 1, 1)
                    add_residual(k * 8 + j, j, 0)
            for s in range(UNITS - 7, UNITS):
                add_residual(s - 1, s - 1, 1)
                add_residual(s, s, 0)
            add_residual(UNITS - 1, UNITS - 1, 1)

        @block.scalar
        def _(act):
            def sizes():
                for k in range(KH):
                    act.wait_ge(w_loaded[k], 16 * QUADS * HALVES)
                    act.activation(w_abs[:, k], w_raw[:, k], ACT.Abs, accum_out=w_sum[:, k:k + 1]
                                   ).then_inc(w_abs_made, 1)

            def sum_kept(rows):
                for k in rows:
                    act.wait_ge(kept_step, 2 * k + 2)
                    act.activation(w_mark[:, k], w_mark[:, k], ACT.Copy, accum_out=kept[:, k, 0:1]
                                   ).then_inc(kept_summed, 1)
                    act.activation(w_abs[:, k], w_abs[:, k], ACT.Copy, accum_out=kept[:, k, 1:2]
                                   ).then_inc(kept_summed, 1)

            def measure(u, j, m):
                t, par = j % QUARTERS, j // QUARTERS % 2
                piece, half = t // 2, t % 2
                rows = xT[:, par, half, 1 + piece * ROWS // 2:1 + (piece + 1) * ROWS // 2, :].rearrange(
                    "p r c -> p (r c)")
                if t == 0 and not (type(u) is int and u == 0):
                    act.wait_ge(ch_stats_ready, m)
                act.wait_ge(x_turned, u + 1)
                if not (type(u) is int and u == 0):
                    act.wait_ge(squared, u)
                act.activation(unread[:, :], rows, ACT.Copy, accum_out=parts[:, 0, half, piece:piece + 1]
                               ).then_inc(x_summed, 1)
                act.wait_ge(x_summed, u + 1)
                if piece == 0:
                    act.mul(neg_shift[:, half:half + 1], parts[:, 0, half, 0:1], -1.0 / PIECE
                            ).then_inc(shifted, 1)
                    act.wait_ge(shifted, 2 * m + 1 + half)
                act.activation(unread[:, :], rows, ACT.Square, bias=neg_shift[:, half:half + 1],
                               accum_out=parts[:, 1, half, piece:piece + 1]).then_inc(squared, 1)

            def high(v, j, half):
                slot = j % ZSLOTS
                act.wait_ge(u_made, 2 * v + half + 1)
                if half == 0:
                    if type(v) is int and v < ZSLOTS:
                        act.wait_ge(pads_made, 1)
                    else:
                        act.wait_ge(mm_done, 8 * v - 8)
                act.activation(Z[:, slot, 0, half, :, 1:COLS + 1], U[:, half], ACT.Copy,
                               scale=scale[:, half:half + 1]).then_inc(hi_made, 1)

            def copy_m1(s, c):
                act.wait_ge(mm_done, 8 * s + 4 * c + 1)
                if not (type(s) is int and 2 * s + c < 1):
                    act.wait_ge(ab_made, 2 * s + c)
                act.activation(m1_sb[:, :], M1[:, c, 0:NPOS], ACT.Copy).then_inc(m1_copied, 1)

            def relu(s, j, c):
                act.wait_ge(y_made, 2 * s + c + 1)
                y = Y[:, c, j % 2 * 2 * NPOS:(j % 2 + 1) * 2 * NPOS]
                act.activation(y, y, ACT.Relu, bias=bias[:, c:c + 1],
                               scale=alpha[:, :]).then_inc(relu_made, 1)

            def step(s, j, image, inside=False):
                do_tin, do_tr, do_mm, do_end = present(s, inside)
                fixed = type(s) is int
                if do_tr and (j + 1) % QUARTERS == 0:
                    act.wait_ge(var_read, image(j + 1) + 1)
                    act.activation(std[:, :], var[:, :], ACT.Sqrt).then_inc(std_made, 1)
                if do_end:
                    relu(s - 1, j - 1, 1)
                if do_mm:
                    copy_m1(s, 0)
                if do_tr:
                    if (j + 1) % QUARTERS == 0:
                        act.wait_ge(stat_step, image(j + 1) * CHAIN + CHAIN)
                    high(s + 1, j + 1, 0)
                if fixed and s == -1:
                    high(0, 0, 1)
                    sum_kept(range(KH))
                if fixed and s == -LEAD:
                    sizes()
                if do_tin:
                    measure(s + LEAD, j + LEAD, image(j + LEAD))
                if do_mm:
                    copy_m1(s, 1)
                if do_tr and not (fixed and s == -1):
                    high(s + 1, j + 1, 1)
                if do_mm:
                    if fixed and s == 0:
                        act.wait_ge(b_loaded, 16 * QUADS)
                        act.wait_ge(alpha_step, 3)
                    relu(s, j, 0)

            for s in range(-LEAD, 1):
                step(s, s, lambda n: n // QUARTERS)
            with act.Fori(0, (UNITS - 8) // 8) as k:
                for j in range(1, 9):
                    step(k * 8 + j, j, lambda n: k * 2 + n // QUARTERS, True)
            for s in range(UNITS - 7, UNITS + 1):
                step(s, s, lambda n: n // QUARTERS)

        @block.vector
        def _(dve):
            def make_threshold():
                dve.wait_ge(w_sums, 1)
                dve.tensor_scalar(thr[:, :], w_totals[:, 0:1], 1.0 / n_weights, THRESHOLD, ALU.mult, ALU.mult
                                  ).then_inc(thr_made, 1)
                dve.wait_ge(thr_made, 1)
                dve.tensor_scalar(neg_thr[:, :], thr[:, :], -1.0, None, ALU.mult).then_inc(thr_made, 1)

            flat = [filt[:, i].rearrange("p b h c e -> p (b h c e)") for i in range(4)]

            def mark_below():
                dve.wait_ge(thr_made, 2)
                for k in range(KH):
                    dve.tensor_scalar(flat[k], w_raw[:, k], neg_thr[:, :], None, ALU.is_le).then_inc(below_made, 1)

            def make_ternary(rows):
                for k in rows:
                    dve.wait_ge(below_made, k + 1)
                    dve.scalar_tensor_tensor(w_ter[:, k], w_raw[:, k], thr[:, :], flat[k],
                                             ALU.is_ge, ALU.subtract).then_inc(ter_made, 1)

            def of_half(row, c):
                return row.rearrange("p (n q c e) -> p n q c e", q=QUADS, c=2, e=QUAD)[:, :, :, c]

            def dst(i, c):
                return filt[:, i, :, :, c].rearrange("p b h (q e) -> p (b h) q e", e=QUAD)

            def make_first_filter():
                dve.wait_ge(ter_made, KH)
                dve.tensor_tensor(flat[3], w_ter[:, 0], w_ter[:, 2], ALU.add).then_inc(filt_step, 1)
                dve.wait_ge(filt_step, 1)
                for c in range(HALVES):
                    ins = dve.tensor_tensor(dst(1, c), of_half(flat[3], c), of_half(w_ter[:, 1], c), ALU.add)
                ins.then_inc(filt_step, 1)

            def make_other_filters():
                for c in range(2):
                    ins = dve.tensor_tensor(dst(2, c), of_half(flat[3], c), of_half(w_ter[:, 1], c), ALU.subtract)
                ins.then_inc(filt_step, 1)
                for c in range(2):
                    ins = dve.tensor_scalar(dst(0, c), of_half(w_ter[:, 0], c), -2.0, None, ALU.mult)
                ins.then_inc(filt_step, 1)
                dve.wait_ge(filt_step, 3)
                for c in range(2):
                    ins = dve.tensor_scalar(dst(3, c), of_half(w_ter[:, 2], c), 2.0, None, ALU.mult)
                ins.then_inc(filt_step, 1)

            def make_alpha():
                dve.wait_ge(w_sums, 2)
                dve.tensor_copy(kept_all[:, :], w_totals[:, 2:4]).then_inc(alpha_step, 1)
                dve.wait_ge(alpha_step, 1)
                dve.reciprocal(inv_n[:, :], kept_all[:, 0:1]).then_inc(alpha_step, 1)
                dve.wait_ge(alpha_step, 2)
                dve.scalar_tensor_tensor(alpha[:, :], kept_all[:, 1:2], 0.5 / SPLIT_SCALE, inv_n[:, :],
                                         ALU.mult, ALU.mult).then_inc(alpha_step, 1)

            def turn(s, u, j):
                t, par = j % QUARTERS, j // QUARTERS % 2
                piece, half, slot = t // 2, t % 2, j // 2 % XSLOTS
                if type(u) is int:
                    loads = u // 2 // XSLOTS + 1
                else:
                    loads = k_of[0] * (8 // 2 // XSLOTS) + (j // 2 // XSLOTS + 1)
                if t % 2 == 0 and not (type(s) is int and s < 1):
                    dve.wait_ge(added, 2 * s - 1)
                dve.wait_ge(x_loaded[slot], loads * (16 * QUADS))
                rows = xT[:, par, half, 1 + piece * ROWS // 2:1 + (piece + 1) * ROWS // 2, :]
                dve.transpose(rows.rearrange("p r c -> p (r c)").rearrange("p (g e) -> p g e", e=QUAD).bitcast(U32),
                              x_in[:, slot, :, half].bitcast(U32)).then_inc(x_turned, 1)

            k_of = [None]

            def stat_sums(m):
                dve.reduce_sum(totals[:, :, :], parts[:, :, :, :], mybir.AxisListType.X).then_inc(stat_step, 1)

            def stat_channel_mean(m):
                dve.wait_ge(stat_step, m * CHAIN + 1)
                dve.tensor_scalar(ch_stats[:, :, 0], totals[:, 0], 1.0 / (ROWS * COLS), None, ALU.mult
                                  ).then_inc(stat_step, 1)

            def stat_offset(m):
                dve.wait_ge(stat_step, m * CHAIN + 2)
                dve.tensor_tensor(off[:, :], ch_stats[:, :, 0], neg_shift[:, :], ALU.add).then_inc(stat_step, 1)

            def stat_offset_squared(m):
                dve.wait_ge(stat_step, m * CHAIN + 3)
                dve.tensor_tensor(off[:, :], off[:, :], off[:, :], ALU.mult).then_inc(stat_step, 1)

            def stat_channel_var(m):
                dve.wait_ge(stat_step, m * CHAIN + 4)
                dve.scalar_tensor_tensor(ch_stats[:, :, 1], totals[:, 1], 1.0 / (ROWS * COLS), off[:, :],
                                         ALU.mult, ALU.subtract).then_inc(ch_stats_ready, 1)

            def stat_group_mean(m):
                dve.wait_ge(group_sums, 2 * m + 1)
                dve.tensor_copy(mean[:, :], M2[:, 0, sums_at:sums_at + HALVES]).then_inc(stat_step, 1)

            def stat_deviation(m):
                dve.wait_ge(stat_step, m * CHAIN + 5)
                dve.tensor_tensor(dev[:, :], ch_stats[:, :, 0], mean[:, :], ALU.subtract).then_inc(stat_step, 1)

            def stat_spread(m):
                dve.tensor_scalar(neg2mean[:, :], mean[:, :], -2.0, None, ALU.mult)
                dve.wait_ge(stat_step, m * CHAIN + 6)
                dve.tensor_tensor(spread[:, :], dev[:, :], dev[:, :], ALU.mult).then_inc(stat_step, 1)
                dve.wait_ge(stat_step, m * CHAIN + 7)
                dve.tensor_tensor(spread[:, :], spread[:, :], ch_stats[:, :, 1], ALU.add).then_inc(spread_ready, 1)

            def fill_edges(par):
                for half in range(HALVES):
                    ins = dve.tensor_scalar(xT[:, par, half, 0:ROWS + 2:ROWS + 1, :],
                                            ones[:, 0:2 * COLS].rearrange("p (r c) -> p r c", r=2),
                                            mean[:, half:half + 1], None, ALU.mult)
                ins.then_inc(edges_made, 1)

            def stat_group_var(m):
                dve.wait_ge(group_sums, 2 * m + 2)
                dve.tensor_scalar(var[:, :], M2[:, 0, sums_at + 8:sums_at + 8 + HALVES], EPS, None, ALU.add
                                  ).then_inc(var_read, 1)

            def scale_inverse(m):
                dve.wait_ge(std_made, m + 1)
                dve.reciprocal(inv0[:, :], std[:, :]).then_inc(stat_step, 1)

            def scale_squared(m):
                dve.wait_ge(stat_step, m * CHAIN + 8)
                dve.tensor_tensor(corr[:, :], inv0[:, :], inv0[:, :], ALU.mult).then_inc(stat_step, 1)

            def scale_end(m):
                at = m * CHAIN
                dve.wait_ge(stat_step, at + 9)
                dve.tensor_tensor(corr[:, :], corr[:, :], var[:, :], ALU.mult).then_inc(stat_step, 1)
                dve.wait_ge(stat_step, at + 10)
                dve.tensor_scalar(corr[:, :], corr[:, :], -0.5 * SPLIT_SCALE, 1.5 * SPLIT_SCALE,
                                  ALU.mult, ALU.add).then_inc(stat_step, 1)
                dve.wait_ge(stat_step, at + 11)
                dve.tensor_tensor(scale[:, :], corr[:, :], inv0[:, :], ALU.mult).then_inc(stat_step, 1)

            def rows_of(j, half):
                row = UROWS * (j % QUARTERS)
                src = xT[:, j // QUARTERS % 2, half]
                return src[:, row + 1:row + 1 + UROWS:2], src[:, row + 2:row + 2 + UROWS:2], src, row

            def differences(v, j, half):
                if not (type(v) is int and v == 0):
                    dve.wait_ge(lo_made, 2 * v + half - 1)
                _, _, src, row = rows_of(j, half)
                dve.tensor_tensor(U[:, half, 0:UROWS].rearrange("p r c -> p (r c)"),
                                  src[:, row + 2:row + 2 + UROWS].rearrange("p r c -> p (r c)"),
                                  src[:, row:row + UROWS].rearrange("p r c -> p (r c)"), ALU.subtract)

            def pair_sums(j, half):
                even, odd, _, _ = rows_of(j, half)
                dve.scalar_tensor_tensor(U[:, half, UROWS:UROWS + PAIRS], even, neg2mean[:, half:half + 1], odd,
                                         ALU.add, ALU.add)

            def pair_differences(j, half):
                even, odd, _, _ = rows_of(j, half)
                dve.tensor_tensor(U[:, half, UROWS + PAIRS:TROWS], odd, even, ALU.subtract).then_inc(u_made, 1)

            def low(v, j, half):
                slot = j % ZSLOTS
                dve.wait_ge(hi_made, 2 * v + half + 1)
                dve.scalar_tensor_tensor(Z[:, slot, 1, half, :, 1:COLS + 1], U[:, half],
                                         scale[:, half:half + 1], Z[:, slot, 0, half, :, 1:COLS + 1],
                                         ALU.mult, ALU.subtract).then_inc(lo_made, 1)

            def sum_m1_m2(s, c):
                dve.wait_ge(m1_copied, 2 * s + c + 1)
                dve.wait_ge(mm_done, 8 * s + 4 * c + 2)
                if not (type(s) is int and 2 * s + c == 0):
                    dve.wait_ge(y_made, 2 * s + c)
                dve.tensor_tensor(AB[:, 0], m1_sb[:, :], M2[:, c, 0:NPOS], ALU.add)

            def difference_m1_m2(c):
                dve.tensor_tensor(AB[:, 1], m1_sb[:, :], M2[:, c, 0:NPOS], ALU.subtract).then_inc(ab_made, 1)

            def join(s, j, c):
                dve.wait_ge(mm_done, 8 * s + 4 * c + 4)
                dve.wait_ge(ab_made, 2 * s + c + 1)
                dve.tensor_tensor(Y[:, c, j % 2 * 2 * NPOS:(j % 2 + 1) * 2 * NPOS].rearrange(
                                      "p (r j c) -> p j r c", j=2, c=COLS),
                                  AB[:, :].rearrange("p j (r c) -> p j r c", c=COLS),
                                  M03[:, c, :, 0:NPOS].rearrange("p j (r c) -> p j r c", c=COLS),
                                  ALU.add).then_inc(y_made, 1)

            def turn_back(s, j, c, stores):
                odd, slot = j % 2, j % OSLOTS
                if c == 0:
                    dve.wait_ge(out_free[slot], stores * (16 * QUADS) + 1)
                dve.wait_ge(added, 2 * s + c + 1)
                first, n = FIRST_GROUP[odd], N_GROUPS[odd]
                dve.transpose(x_out[:, slot, 0:n, c].bitcast(U32),
                              Y[:, c, QUAD * first:QUAD * (first + n)].rearrange("p (g e) -> p g e", e=QUAD
                                                                                ).bitcast(U32)
                              ).then_inc(turned_back, 1)

            def step(s, j, image, inside=False):
                do_tin, do_tr, do_mm, do_end = present(s, inside)
                fixed = type(s) is int
                u, v = s + LEAD, s + 1
                m = image(j + 2)
                new = do_tin and (j + LEAD) % QUARTERS == QUARTERS - 1
                first_unit = do_tr and (j + 1) % QUARTERS == 0
                m_first = image(j + 1)
                stores = (s - 1) // OSLOTS if fixed else k_of[0] * (8 // OSLOTS) + (j - 1) // OSLOTS
                if first_unit:
                    stat_group_var(m_first)
                if do_end:
                    join(s - 1, j - 1, 1)
                if do_tr:
                    if first_unit:
                        dve.wait_ge(edges_made, m_first + 1)
                        dve.wait_ge(spread_ready, m_first + 1)
                    differences(v, j + 1, 0)
                    if first_unit:
                        scale_inverse(m_first)
                    pair_sums(j + 1, 0)
                    if first_unit:
                        scale_squared(m_first)
                    pair_differences(j + 1, 0)
                    if first_unit:
                        scale_end(m_first)
                if do_end:
                    turn_back(s - 1, j - 1, 0, stores)
                if fixed and s == -1:
                    differences(0, 0, 1)
                    pair_sums(0, 1)
                    pair_differences(0, 1)
                    low(0, 0, 0)
                    low(0, 0, 1)
                    make_other_filters()
                    do_tr = False
                if do_tin:
                    turn(s, u, j + LEAD)
                if fixed and s == 1 - LEAD:
                    make_threshold()
                    mark_below()
                    make_ternary(range(2))
                if fixed and s == 3 - LEAD:
                    make_ternary(range(2, KH))
                    make_first_filter()
                if do_end:
                    turn_back(s - 1, j - 1, 1, stores)
                if do_mm:
                    sum_m1_m2(s, 0)
                    difference_m1_m2(0)
                if do_tr:
                    low(v, j + 1, 0)
                if new:
                    dve.wait_ge(squared, u + 1)
                    stat_sums(m)
                if do_tr:
                    differences(v, j + 1, 1)
                if new:
                    stat_channel_mean(m)
                if do_tr:
                    pair_sums(j + 1, 1)
                if new:
                    stat_offset(m)
                if do_tr:
                    pair_differences(j + 1, 1)
                if new:
                    stat_offset_squared(m)
                    stat_channel_var(m)
                if do_mm:
                    join(s, j, 0)
                if fixed and s == 0:
                    make_alpha()
                if do_mm:
                    sum_m1_m2(s, 1)
                    difference_m1_m2(1)
                if new:
                    stat_group_mean(m)
                if new:
                    stat_deviation(m)
                if do_tr:
                    low(v, j + 1, 1)
                if new:
                    stat_spread(m)
                    fill_edges((j + 2) // QUARTERS % 2)

            for s in range(-LEAD, 1):
                step(s, s, lambda n: n // QUARTERS)
            with dve.Fori(0, (UNITS - 8) // 8) as k:
                k_of[0] = k
                for j in range(1, 9):
                    step(k * 8 + j, j, lambda n: k * 2 + n // QUARTERS, True)
            for s in range(UNITS - 7, UNITS + 1):
                step(s, s, lambda n: n // QUARTERS)

        @block.tensor
        def _(pe):
            pe.wait_ge(consts_made, 4)

            def sum_sizes():
                for k in range(KH):
                    pe.wait_ge(w_abs_made, k + 1)
                    ins = pe.matmul(w_totals[:, 0:1], ones[:, :], w_sum[:, k:k + 1],
                                    start=k == 0, stop=k == KH - 1)
                ins.then_inc(w_sums, 1)

            def product(s, j, c, i):
                before = 2 * s + c - 1
                if i == 1:
                    target, free = M1[:, c, 0:NPOS], m1_copied
                elif i == 2:
                    target, free = M2[:, c, 0:NPOS], ab_made
                else:
                    target, free = M03[:, c, i // 3, 0:NPOS], y_made
                if i != 3 and not (type(before) is int and before < 1):
                    pe.wait_ge(free, before)
                n = 0
                for kw in range(KW):
                    for half in range(HALVES):
                        for part in range(2):
                            first, row_step = FIRST_ROW[i], ROW_STEP[i]
                            ins = pe.matmul(target, filt[:, i, kw, half, c],
                                            Z[:, j % ZSLOTS, part, half,
                                              first:first + row_step * (PAIRS - 1) + 1:row_step, kw:kw + COLS],
                                            start=n == 0, stop=n == 2 * KW * HALVES - 1)
                            n += 1
                ins.then_inc(mm_done, 1)

            def step(s, j, image, inside=False):
                do_tin, do_tr, do_mm, do_end = present(s, inside)
                fixed = type(s) is int
                last_quarter = do_tin and (j + LEAD) % QUARTERS == QUARTERS - 1
                if do_mm:
                    pe.wait_ge(hi_made, 2 * s + 2)
                    pe.wait_ge(lo_made, 2 * s + 2)
                if fixed and s == 1 - LEAD:
                    sum_sizes()
                for g in range(8):
                    if fixed and s == 0 and g < 4:
                        pe.wait_ge(filt_step, g + 2)
                    if fixed and s == 0 and g == 7:
                        pe.wait_ge(alpha_step, 1)
                    if do_tr and g == 1 and (j + 1) % QUARTERS == 0:
                        pe.wait_ge(var_read, image(j + 1) + 1)
                    if do_mm:
                        product(s, j, g // 4, FILTER[g % 4])
                    if fixed and s == 0 and g == 4:
                        pe.wait_ge(kept_summed, 2 * KH)
                        for k in range(KH):
                            ins = pe.matmul(w_totals[:, 2:4], ones[:, :], kept[:, k], start=k == 0, stop=k == KH - 1)
                        ins.then_inc(w_sums, 1)
                    if last_quarter and g == MEAN_GAP:
                        pe.wait_ge(ch_stats_ready, image(j + 2) + 1)
                        if do_mm:
                            pe.wait_ge(ab_made, 2 * s + 1)
                        pe.matmul(M2[:, 0, sums_at:sums_at + HALVES], group_avg[:, :], ch_stats[:, :, 0],
                                  start=True, stop=True).then_inc(group_sums, 1)
                    if last_quarter and g == VAR_GAP:
                        pe.wait_ge(spread_ready, image(j + 2) + 1)
                        pe.matmul(M2[:, 0, sums_at + 8:sums_at + 8 + HALVES], group_avg[:, :], spread[:, :],
                                  start=True, stop=True).then_inc(group_sums, 1)

            for s in range(-LEAD, 1):
                step(s, s, lambda n: n // QUARTERS)
            with pe.Fori(0, (UNITS - 8) // 8) as k:
                for j in range(1, 9):
                    step(k * 8 + j, j, lambda n: k * 2 + n // QUARTERS, True)
            for s in range(UNITS - 7, UNITS + 1):
                step(s, s, lambda n: n // QUARTERS)


def kernel(x, L0_conv_W, L0_conv_b):
    import numpy as _np
    import concourse.bacc as _bacc
    from concourse.bass_utils import run_bass_kernel_spmd as _run

    nc = _bacc.Bacc("TRN2", target_bir_lowering=False, num_devices=1)
    arrays, args = {}, []
    for name, a in (("x", x), ("w", L0_conv_W), ("b", L0_conv_b)):
        a = _np.ascontiguousarray(a)
        arrays[name] = a
        args.append(nc.dram_tensor(name, a.shape, mybir.dt.from_np(a.dtype), kind="ExternalInput").ap())
    args.append(nc.dram_tensor("out", arrays["x"].shape, F32, kind="ExternalOutput").ap())
    build(nc, *args)
    return _run(nc, [arrays], core_ids=[0]).results[0]["out"]
```
